# Optimizing a Trainium2 kernel written in Bass

```python
import numpy as np
import jax
import jax.numpy as jnp

def _softmax(x, axis=-1):
    return jax.nn.softmax(x, axis=axis)

def _gelu(x):
    return jax.nn.gelu(x, approximate=True)

def _silu(x):
    return jax.nn.silu(x)

def _sigmoid(x):
    return jax.nn.sigmoid(x)

def _layernorm(x, axis=-1, eps=1e-05):
    m = jnp.mean(x, axis=axis, keepdims=True)
    v = jnp.var(x, axis=axis, keepdims=True)
    return (x - m) / jnp.sqrt(v + eps)

def _scatter_add(tgt, idx, src, axis=0):
    return tgt.at[idx].add(src)

def _segment_sum(src, seg, n):
    return jax.ops.segment_sum(src, seg, n)
kernel_name = 'mk_gnn_preln_d1_gnn_r8_8f3944'

def setup_inputs(seed: int=0):
    np.random.seed(seed)
    _w = jnp.asarray

    def _rec_inputs():
        import jax
        import jax.numpy as jnp
        _gk = jax.random.key(seed)
        x = -0.0003929 + 0.9999 * jax.random.normal(jax.random.fold_in(_gk, 1), (1250, 512), jnp.float32)
        src = jax.random.randint(jax.random.fold_in(_gk, 2), (40000,), 0, 1250, jnp.int32)
        dst = jnp.minimum((1250 * jax.random.uniform(jax.random.fold_in(_gk, 3), (40000,)) ** 2.0).astype(jnp.int32), 9999)
        _o = jnp.argsort(dst, stable=True)
        src = src[_o]
        dst = dst[_o]
        return (x, src, dst)
    x, src, dst = _rec_inputs()

    def _L0_gnn_setup():
        import jax, jax.numpy as jnp
        import numpy as np
        N_NODES = 4096
        N_EDGES = 32768
        D = 512
        NUM_EXPERTS = 4
        TOP_K = 2
        LAYERS = 2
        key = jax.random.key(seed)
        ks = jax.random.split(key, 8)
        x = jax.random.normal(ks[0], (N_NODES, D), dtype=jnp.float32)
        edge_index = jax.random.randint(ks[1], (2, N_EDGES), 0, N_NODES, dtype=jnp.int64)
        s = 1.0 / np.sqrt(D)
        gate_W = jax.random.uniform(ks[2], (D, NUM_EXPERTS), jnp.float32, -s, s)
        gate_b = jax.random.uniform(ks[3], (NUM_EXPERTS,), jnp.float32, -s, s)
        Wl = jax.random.uniform(ks[4], (NUM_EXPERTS, LAYERS, D, D), jnp.float32, -s, s)
        bl = jax.random.uniform(ks[5], (NUM_EXPERTS, LAYERS, D), jnp.float32, -s, s)
        Wr = jax.random.uniform(ks[6], (NUM_EXPERTS, LAYERS, D, D), jnp.float32, -s, s)
        return {'x': x, 'gate_W': gate_W, 'gate_b': gate_b, 'Wl': Wl, 'bl': bl, 'Wr': Wr, 'edge_index': edge_index}
    _L0_gnn_all = _L0_gnn_setup()
    _L0_gnn_in = {k: v for k, v in _L0_gnn_all.items() if k in ('gate_W', 'gate_b', 'Wl', 'bl', 'Wr')}
    del _L0_gnn_all
    return {'x': x, 'src': src, 'dst': dst, 'L0_gnn_gate_W': _L0_gnn_in['gate_W'], 'L0_gnn_gate_b': _L0_gnn_in['gate_b'], 'L0_gnn_Wl': _L0_gnn_in['Wl'], 'L0_gnn_bl': _L0_gnn_in['bl'], 'L0_gnn_Wr': _L0_gnn_in['Wr']}

def reference(x, src, dst, L0_gnn_gate_W, L0_gnn_gate_b, L0_gnn_Wl, L0_gnn_bl, L0_gnn_Wr):
    import jax
    import jax.numpy as jnp

    def _L0_gnn_ref(x, gate_W, gate_b, Wl, bl, Wr, edge_index):
        import jax, jax.numpy as jnp
        import numpy as np
        N_NODES = 4096
        N_EDGES = 32768
        D = 512
        NUM_EXPERTS = 4
        TOP_K = 2
        LAYERS = 2
        n = x.shape[0]
        src, dst = (edge_index[0], edge_index[1])
        gates = jax.nn.softmax(x @ gate_W + gate_b, axis=-1)
        top_v, top_i = jax.lax.top_k(gates, TOP_K)
        deg = jax.ops.segment_sum(jnp.ones((src.shape[0],), x.dtype), dst, num_segments=n)
        inv_deg = jnp.where(deg > 0, 1.0 / jnp.maximum(deg, 1.0), 0.0)[:, None]

        def sage_conv(h, W_l, b_l, W_r):
            aggr = jax.ops.segment_sum(h[src], dst, num_segments=n) * inv_deg
            return aggr @ W_l + b_l + h @ W_r
        expert_outs = []
        for e in range(NUM_EXPERTS):
            h = x
            for l in range(LAYERS):
                h = sage_conv(h, Wl[e, l], bl[e, l], Wr[e, l])
                h = jax.nn.relu(h)
            expert_outs.append(h)
        expert_outputs = jnp.stack(expert_outs, axis=1)
        sel = jnp.take_along_axis(expert_outputs, top_i[:, :, None], axis=1)
        out = jnp.sum(sel * top_v[:, :, None], axis=1)
        return out
    edge_index = jnp.stack([src, dst])
    h = jnp.maximum(_layernorm(x, axis=-1), 0.0)
    x = x + _L0_gnn_ref(h, L0_gnn_gate_W, L0_gnn_gate_b, L0_gnn_Wl, L0_gnn_bl, L0_gnn_Wr, edge_index)
    return x

_drawn_inputs = setup_inputs


def setup_inputs(seed=0):
    import zlib

    import numpy as np

    out = dict(_drawn_inputs(seed))
    spreads = {}
    factors = {'L0_gnn_gate_b': 4.584, 'L0_gnn_bl': 6.056}
    for name, (base, spread) in spreads.items():
        noise = np.random.default_rng([zlib.crc32(name.encode()), seed]).standard_normal(out[name].shape)
        drawn = base * np.exp(spread * noise) if base else spread * noise
        out[name] = jnp.asarray(drawn.astype(out[name].dtype))
    for name, factor in factors.items():
        out[name] = (out[name] * factor).astype(out[name].dtype)
    return out
```

```python
from contextlib import ExitStack

import concourse.bass as bass
from concourse import mybir

ALU = mybir.AluOpType
ACT = mybir.ActivationFunctionType
AX = mybir.AxisListType
F32 = mybir.dt.float32
F16 = mybir.dt.float16
F8 = mybir.dt.float8e4
I32 = mybir.dt.int32
U8 = mybir.dt.uint8

P = 128
WIN = 48
CREDIT = 1
SLOTS = 4
HSCALE = 1024.0
YSCALE = 2.0 ** -24
EXP1 = 1 << 23
TINY = 2.0 ** -60


def sage_moe_kernel(nc, x, src, dst, gate_W, gate_b, Wl, bl, Wr, out):
    N, D = x.shape
    E, L = Wl.shape[0], Wl.shape[1]
    NE = src.shape[0]
    FC = D // P
    NT = (N + P - 1) // P
    ROWS = [min(P, N - t * P) for t in range(NT)]
    TAIL = ROWS[-1]
    CH = 5
    EP = 125
    EG = CH * EP
    G = NE // EG
    assert G * EG == NE and G == 64 and G % SLOTS == 0
    AW = NT * WIN
    assert AW <= 512
    NWIN = (N + WIN - 1) // WIN
    CW = 1300
    assert CW >= N - 1 + WIN and CW >= NWIN * WIN
    NC = [(0, 417), (417, 417), (834, 416)]
    NCW = 417
    L0 = FC * len(NC)
    RING = L0 + NT
    assert RING - SLOTS >= L0 and L0 % 2 == 0 and NT % 2 == 0

    with ExitStack() as ctx:
        def sb(name, shape, dt):
            return ctx.enter_context(nc.sbuf_tensor(name, shape, dt))

        def psum(name, shape, dt=F32):
            return ctx.enter_context(nc.psum_tensor(name, shape, dt))

        def sem(name):
            return ctx.enter_context(nc.semaphore(name))

        ring = [psum(f"ring{i}", [P, 512]) for i in range(SLOTS)]
        ps_z = [psum(f"ps_z{i}", [P, 512]) for i in range(2)]
        ps_a = [psum(f"ps_a{i}", [P, 512]) for i in range(2)]

        C = sb("C", [P, NT * CW], F16)
        C_rest = sb("C_rest", [P, NT * CW], F8)
        hT = sb("hT", [P, 2, FC, N], F16)
        aT = sb("aT", [P, 2, FC, N], F16)
        h1T = sb("h1T", [P, 2, FC, N], F16)
        W16 = sb("W16", [P, L, 2, 2, FC, D], F16)
        W32 = sb("W32", [P, 2, FC * D], F32)
        acc = sb("acc", [P, NT, D], F32)
        y = sb("y", [P, 2, NT, D], F16)
        tmp32 = sb("tmp32", [P, 2, NCW], F32)
        inv_bc = sb("inv_bc", [P, N], F32)
        bias1 = sb("bias1", [P, D], F32)
        zt = sb("zt", [P, 3, D], F32)
        ident = sb("ident", [P, P], F32)
        ones16 = sb("ones16", [P, P], F16)
        iota_i = zt.ap().rearrange("p a d -> p (a d)")[:, 0:AW].bitcast(I32)
        iota16 = sb("iota16", [P, AW], F16)
        minmax = sb("minmax", [G, 2], F32)
        dst_c, shi_c, slo_c = (inv_bc[0:EP, k * CH * G:(k + 1) * CH * G].rearrange("p (c g) -> p c g", c=CH)
                               for k in range(3))
        col_c = sb("col_c", [EP, CH, G], F32)
        row = sb("row", [P, 2, G], F32)
        base_i = sb("base_i", [1, G], I32)
        chk = sb("chk", [1, 3, G], F32)
        chk3 = sb("chk3", [1, 8], F32)
        flag_i = sb("flag_i", [1, 1], I32)
        stats = sb("stats", [P, NT, 6], F32)
        mv = sb("mv", [P, NT, 2], F32)
        rs = sb("rs", [P, 4, NT], F32)
        gW = sb("gW", [P, FC, E], F32)
        gb = sb("gb", [P, E], F32)
        logit = sb("logit", [P, NT, E], F32)
        wins = sb("wins", [P, NT, E], F32)
        beat = sb("beat", [P, 2, NT], F32)
        gmax = sb("gmax", [P, NT, 1], F32)
        gsum = sb("gsum", [P, NT, 1], F32)
        gate = sb("gate", [P, E, NT], F32)
        gate_now = sb("gate_now", [P, NT], F32)
        inv_col = sb("inv_col", [P, NT], F32)
        inv_s = sb("inv_s", [P, NT], F32)
        b_rows = sb("b_rows", [E * FC, P], F32)
        b0T = sb("b0T", [P, E * FC], F32)
        bmax = sb("bmax", [P, E], F32)
        bmaxA = sb("bmaxA", [P, E], F32)
        bs = sb("bs", [P, FC], F32)
        wmax = sb("wmax", [P, 1], F32)
        wmaxA = sb("wmaxA", [P, 1], F32)
        sc = sb("sc", [P, 12], F32)
        done_mark = sb("done_mark", [1, 8], F32)

        hotA = aT.ap().rearrange("p a c n -> p (a c n)")[0:EP, 0:SLOTS * CH * AW].rearrange(
            "p (u c a) -> p u c a", u=SLOTS, c=CH)
        hotB = W16.ap()[:, 1].rearrange("p a b c d -> p (a b c d)")[0:EP, 0:SLOTS * CH * P].rearrange(
            "p (u c b) -> p u c b", u=SLOTS, c=CH)
        w32_flat = W32.ap().rearrange("p a b -> p (a b)")

        def edge_tmp(k):
            return w32_flat[0:G, k * EG:(k + 1) * EG]

        dst_i, src_i, dst_f, shi_f, slo_f = (edge_tmp(k) for k in range(5))
        shi_i = edge_tmp(5)
        mm_bc = w32_flat[0:G, 6 * EG:6 * EG + 2 * EP].rearrange("p (k e) -> p k e", k=2)
        hT32 = h1T.ap().rearrange("p a c n -> p (a c n)").bitcast(F32).rearrange("p (c n) -> p c n", c=FC)
        h32 = zt
        near16 = zt.ap()[:, 1, 0:AW // 2].bitcast(F16).rearrange("p (t n) -> p t n", n=WIN)
        rest8 = zt.ap()[:, 2, 0:AW // 4].bitcast(F8).rearrange("p (t n) -> p t n", n=WIN)
        C3 = C.ap().rearrange("p (t n) -> p t n", t=NT)
        R3 = C_rest.ap().rearrange("p (t n) -> p t n", t=NT)

        names = ("dst_in src_in consts_in w_in b1_in out_done edges_split edges_T win_ready"
                 " ident_ready iota_ready iotas_cast C_zero ones_ready flag_ready dve"
                 " bn_done sqrt_done h1_scale_ready xn_ready h32_ready h16hi_ready h16lo_ready hT_ps hT32_ready hThi_ready hTlo_ready"
                 " gates_ps b0_ps b0_ready exp_done gates_done"
                 " hot_ready counted added slow_hot slow_counted slow_read slow_evac C_ready"
                 " deg_ps inv_ready invcol_ps invcol_ready"
                 " ring_full agg0_scaled agg0_hi agg0_lo"
                 " wmax_ready wmax_all scale_ready Whi_ready Wlo_ready"
                 " l0_read l0_lo y_hi y_lo z_full a_full z_read t_ready relu_ready tile_done bmax_ready bmax_all").split()
        S = {n: sem(n) for n in names}
        x_in = [sem(f"x_in{j}") for j in range(NT // 2)]

        x_rows = x.rearrange("(o n) d -> o n d", o=1)
        Wl_q = Wl.rearrange("e l (c p) d -> (e l) p c d", p=P)
        Wr_q = Wr.rearrange("e l (c p) d -> (e l) p c d", p=P)
        W32v = W32.ap().rearrange("p a (c d) -> p a c d", c=FC)
        QN = E * L

        block = ctx.enter_context(nc.Block())

        @block.sync
        def _(sp):
            sp.dma_start(dst_i.bitcast(I32), dst.rearrange("(g e) -> g e", e=EG)).then_inc(S["dst_in"], 16)
            sp.dma_start(src_i.bitcast(I32), src.rearrange("(g e) -> g e", e=EG)).then_inc(S["src_in"], 16)
            for j in range(NT // 2):
                t = 2 * j
                if ROWS[t + 1] == P:
                    sp.dma_start(acc[:, t:t + 2, :], x[t * P:(t + 2) * P, :].rearrange("(a p) d -> p a d", p=P)
                                 ).then_inc(x_in[j], 16)
                else:
                    sp.dma_start(acc[:, t, :], x[t * P:(t + 1) * P, :]).then_inc(x_in[j], 16)
                    sp.dma_start(acc[0:TAIL, t + 1, :], x[(t + 1) * P:N, :]).then_inc(x_in[j], 16)
            sp.dma_start(gW[:], gate_W.rearrange("(c p) e -> p c e", p=P)).then_inc(S["consts_in"], 16)
            sp.dma_start(gb[:], gate_b.partition_broadcast(P)).then_inc(S["consts_in"], 16)
            for e in range(E):
                sp.dma_start(b_rows[e * FC:(e + 1) * FC, :], bl[e, 0, :].rearrange("(c p) -> c p", p=P)
                             ).then_inc(S["consts_in"], 16)
            sp.wait_ge(S["edges_T"], 1)
            sp.dma_start(W32v[:, 0], Wl_q[0]).then_inc(S["w_in"], 16)
            sp.dma_start(W32v[:, 1], Wr_q[0]).then_inc(S["w_in"], 16)

            def expert_loads(e, last):
                sp.wait_ge(S["Whi_ready"], e * 2 + 1)
                sp.wait_ge(S["Wlo_ready"], e * 2 + 1)
                sp.dma_start(W32v[:, 0], Wl_q[bass.ds(e * 2 + 1, 1)].rearrange("o p c d -> p (o c) d")
                             ).then_inc(S["w_in"], 16)
                sp.dma_start(W32v[:, 1], Wr_q[bass.ds(e * 2 + 1, 1)].rearrange("o p c d -> p (o c) d")
                             ).then_inc(S["w_in"], 16)
                sp.wait_ge(S["z_read"], CREDIT + e * NT)
                sp.dma_start(bias1[:], bl[bass.ds(e, 1), 1, :].rearrange("a d -> (a d)").partition_broadcast(P)
                             ).then_inc(S["b1_in"], 16)
                sp.wait_ge(S["Whi_ready"], e * 2 + 2)
                sp.wait_ge(S["Wlo_ready"], e * 2 + 2)
                if not last:
                    sp.dma_start(W32v[:, 0], Wl_q[bass.ds(e * 2 + 2, 1)].rearrange("o p c d -> p (o c) d")
                                 ).then_inc(S["w_in"], 16)
                    sp.dma_start(W32v[:, 1], Wr_q[bass.ds(e * 2 + 2, 1)].rearrange("o p c d -> p (o c) d")
                                 ).then_inc(S["w_in"], 16)

            with sp.Fori(0, E - 1) as e:
                expert_loads(e, False)
            expert_loads(E - 1, True)
            for t in range(NT):
                sp.wait_ge(S["tile_done"], CREDIT + (E - 1) * NT + t + 1)
                sp.dma_start(out[t * P:t * P + ROWS[t], :], acc[0:ROWS[t], t, :]).then_inc(S["out_done"], 16)
            sp.wait_ge(S["out_done"], 16 * NT)

        @block.gpsimd
        def _(pool):
            nc.gpsimd.memset(ident[:], 0.0).then_inc(S["ident_ready"], 1)
            pool.wait_ge(S["ident_ready"], 1)
            nc.gpsimd.affine_select(out=ident[:], in_=ident[:], compare_op=ALU.not_equal, fill=1.0, base=0,
                                    pattern=[[-1, P]], channel_multiplier=1).then_inc(S["ident_ready"], 1)
            nc.gpsimd.iota(iota_i, pattern=[[1, AW]], base=0, channel_multiplier=0).then_inc(S["iota_ready"], 1)
            nc.gpsimd.memset(C.ap().bitcast(F32), 0.0).then_inc(S["C_zero"], 1)
            pool.wait_ge(S["bmax_ready"], 1)
            nc.gpsimd.partition_all_reduce(bmaxA[:], bmax[:], P, bass.bass_isa.ReduceOp.max
                                           ).then_inc(S["bmax_all"], 1)
            for q in range(QN):
                pool.wait_ge(S["wmax_ready"], q + 1)
                nc.gpsimd.partition_all_reduce(wmaxA[:], wmax[:], P, bass.bass_isa.ReduceOp.max
                                               ).then_inc(S["wmax_all"], 1)

        @block.scalar
        def _(act):
            act.wait_ge(S["bn_done"], 1)
            nc.scalar.activation(rs[:, 1, :], rs[:, 0, :], ACT.Sqrt).then_inc(S["sqrt_done"], 1)
            for t in range(NT):
                r = ROWS[t]
                act.wait_ge(S["xn_ready"], t + 1)
                if t >= 2:
                    act.wait_ge(S["h16lo_ready"], t - 1)
                    act.wait_ge(S["hT_ps"], t - 1)
                nc.scalar.activation(h32[0:r, t % 2, :], h32[0:r, t % 2, :], ACT.Relu).then_inc(S["h32_ready"], 1)
                act.wait_ge(S["h32_ready"], t + 1)
                nc.scalar.activation(y[0:r, 0, t, :], h32[0:r, t % 2, :], ACT.Copy, scale=HSCALE
                                     ).then_inc(S["h16hi_ready"], 1)
                act.wait_ge(S["hT_ps"], t + 1)
                pv = ps_z[t % 2][:, :].rearrange("p (c n) -> p c n", c=FC)[:, :, 0:r]
                nc.scalar.activation(hT32[:, :, t * P:t * P + r], pv, ACT.Copy).then_inc(S["hT32_ready"], 1)
                nc.scalar.activation(hT[:, 0, :, t * P:t * P + r], pv, ACT.Copy, scale=HSCALE
                                     ).then_inc(S["hThi_ready"], 1)
            act.wait_ge(S["gates_done"], 1)
            nc.scalar.activation(logit[:], logit[:], ACT.Exp).then_inc(S["exp_done"], 1)

            def split_hi(q, l):
                act.wait_ge(S["scale_ready"], q + 1)
                nc.scalar.activation(W16[:, l, 0, :, :, :].rearrange("p a c d -> p (a c d)"), w32_flat,
                                     ACT.Copy, scale=sc[:, 3 * l:3 * l + 1]).then_inc(S["Whi_ready"], 1)

            for i in range(L0):
                c, (n0, w) = i // len(NC), NC[i % len(NC)]
                if i == 1:
                    split_hi(0, 0)
                act.wait_ge(S["agg0_scaled"], i + 1)
                nc.scalar.activation(aT[:, 0, c, n0:n0 + w], tmp32[:, i % 2, 0:w], ACT.Copy
                                     ).then_inc(S["agg0_hi"], 1)

            def expert(e, last):
                for i in range(L0):
                    c, (n0, w) = i // len(NC), NC[i % len(NC)]
                    act.wait_ge(S["ring_full"], L0 + e * RING + i + 1)
                    if i == 0:
                        act.wait_ge(S["l0_lo"], e * L0 + L0)
                    elif i >= 2:
                        act.wait_ge(S["l0_lo"], e * L0 + L0 + i - 1)
                    if i == 0:
                        act.wait_ge(S["h1_scale_ready"], e + 1)
                        act.wait_ge(S["t_ready"], CREDIT + e * NT)
                    nc.scalar.activation(tmp32[:, i % 2, 0:w], ring[i % SLOTS][:, 0:w], ACT.Relu,
                                         bias=bs[:, c:c + 1], scale=sc[:, 6:7])
                    nc.scalar.activation(h1T[:, 0, c, n0:n0 + w], ring[i % SLOTS][:, 0:w], ACT.Relu,
                                         bias=bs[:, c:c + 1], scale=sc[:, 6:7]).then_inc(S["l0_read"], 1)
                    if i == 2:
                        split_hi(e * 2 + 1, 1)
                for t in range(NT):
                    i, r = L0 + t, ROWS[t]
                    act.wait_ge(S["ring_full"], L0 + e * RING + i + 1)
                    nc.scalar.activation(y[0:r, 0, t, :], ring[i % SLOTS][0:r, :], ACT.Copy, scale=YSCALE
                                         ).then_inc(S["y_hi"], 1)
                for t in range(NT):
                    r = ROWS[t]
                    act.wait_ge(S["t_ready"], CREDIT + e * NT + t + 1)
                    nc.scalar.activation(zt[0:r, t % 3, :], zt[0:r, t % 3, :], ACT.Relu,
                                         scale=gate_now[0:r, t:t + 1]).then_inc(S["relu_ready"], 1)
                    if t == 2 and not last:
                        split_hi(e * 2 + 2, 0)

            with act.Fori(0, E - 1) as e:
                expert(e, False)
            expert(E - 1, True)

        def slow_columns(dve, V, w):
            def then(ins, k):
                ins.then_inc(S["slow_evac"], 1)
                dve.wait_ge(S["slow_evac"], w * 6 + k)
            inside = zt[0:EP, 0, 0:CH * G].rearrange("p (c g) -> p c g", c=CH)
            below = zt[0:EP, 1, 0:CH * G].rearrange("p (c g) -> p c g", c=CH)
            V.tensor_scalar(below, dst_c, float(WIN), None, ALU.is_lt)
            then(V.tensor_scalar(inside, dst_c, 0.0, None, ALU.is_ge), 1)
            V.tensor_tensor(inside, inside, below, ALU.mult)
            then(V.scalar_tensor_tensor(out=col_c[:], in0=shi_c, scalar=float(WIN), in1=dst_c,
                                        op0=ALU.mult, op1=ALU.add), 2)
            V.scalar_tensor_tensor(out=col_c[:], in0=col_c[:], scalar=1.0, in1=inside,
                                   op0=ALU.add, op1=ALU.mult)
            then(V.tensor_scalar(dst_c, dst_c, -float(WIN), None, ALU.add), 3)
            then(V.tensor_scalar(col_c[:], col_c[:], -1.0, None, ALU.add), 4)

        @block.vector
        def _(dve):
            chain = [0]

            def link(ins):
                chain[0] += 1
                ins.then_inc(S["dve"], 1)
                dve.wait_ge(S["dve"], chain[0])

            V = nc.vector
            for k, n in enumerate(("y_lo", "t_ready", "tile_done", "z_read", "slow_read", "added")):
                V.memset(done_mark[:, k + 2:k + 3], 0.0).then_inc(S[n], CREDIT)
            V.memset(ones16[:], 1.0)
            V.memset(mv[:], 1.0)
            V.memset(logit[:], 0.0)
            V.memset(inv_col[:], 0.0).then_inc(S["ones_ready"], 1)
            dve.wait_ge(S["iota_ready"], 1)
            V.tensor_copy(iota16[:], iota_i).then_inc(S["iotas_cast"], 1)

            dve.wait_ge(S["dst_in"], 16)
            link(V.tensor_copy(dst_f, dst_i.bitcast(I32)))
            V.tensor_reduce(minmax[:, 0:1], dst_f, AX.X, ALU.min)
            link(V.tensor_reduce(minmax[:, 1:2], dst_f, AX.X, ALU.max))
            dve.wait_ge(S["src_in"], 16)
            link(V.tensor_scalar(shi_i.bitcast(I32), src_i.bitcast(I32), 7, None, ALU.logical_shift_right))
            link(V.tensor_copy(shi_f, shi_i.bitcast(I32)))
            link(V.tensor_scalar(shi_i.bitcast(I32), src_i.bitcast(I32), P - 1, None, ALU.bitwise_and))
            link(V.memset(mm_bc, 0.0))
            V.tensor_scalar(mm_bc[:, 0, :], mm_bc[:, 0, :], minmax[:, 0:1], None, ALU.add)
            V.tensor_scalar(mm_bc[:, 1, :], mm_bc[:, 1, :], minmax[:, 1:2], None, ALU.add)
            V.tensor_copy(slo_f, shi_i.bitcast(I32)).then_inc(S["edges_split"], 1)

            dve.wait_ge(S["edges_T"], 1)
            pc = [ring[k][0:EP, 0:CH * G].rearrange("p (c g) -> p c g", c=CH) for k in range(3)]
            V.tensor_copy(row[0:EP, 0, :], ring[3][0:EP, 0:G])
            V.tensor_copy(row[0:EP, 1, :], ring[3][0:EP, G:2 * G])
            V.tensor_copy(dst_c, pc[0])
            V.tensor_copy(shi_c, pc[1])
            link(V.tensor_copy(slo_c, pc[2]))
            V.tensor_copy(base_i[:], row[0:1, 0, :])
            link(V.scalar_tensor_tensor(out=col_c[:], in0=shi_c, scalar=float(WIN), in1=dst_c,
                                        op0=ALU.mult, op1=ALU.add))
            V.tensor_tensor(col_c[:], col_c[:], row[0:EP, 0:1, :].to_broadcast([EP, CH, G]), ALU.subtract)
            mn, mx = row[0:1, 0, :], row[0:1, 1, :]
            V.tensor_tensor(chk[:, 0, :], mx, mn, ALU.subtract)
            V.tensor_tensor(chk[:, 1, 0:G - 1], mx[:, 0:G - 1], mn[:, 1:G], ALU.subtract)
            link(V.tensor_tensor(chk[:, 2, 0:G - 3], mx[:, 0:G - 3], mn[:, 3:G], ALU.subtract))
            V.tensor_reduce(chk3[:, 0:1], chk[:, 0, :], AX.X, ALU.max)
            V.tensor_reduce(chk3[:, 1:2], chk[:, 1, 0:G - 1], AX.X, ALU.max)
            link(V.tensor_reduce(chk3[:, 2:3], chk[:, 2, 0:G - 3], AX.X, ALU.max))
            V.tensor_scalar(chk3[:, 3:4], chk3[:, 0:1], float(WIN), None, ALU.is_ge)
            V.tensor_scalar(chk3[:, 4:5], chk3[:, 1:2], 0.0, None, ALU.is_gt)
            link(V.tensor_scalar(chk3[:, 5:6], chk3[:, 2:3], 0.0, None, ALU.is_ge))
            link(V.tensor_reduce(chk3[:, 6:7], chk3[:, 3:6], AX.X, ALU.max))
            V.tensor_copy(flag_i[:], chk3[:, 6:7]).then_inc(S["flag_ready"], 1)

            for t in range(NT):
                r = ROWS[t]
                if t % 2 == 0:
                    dve.wait_ge(x_in[t // 2], 16 if ROWS[t + 1] == P else 32)
                ins = V.bn_stats(stats[0:r, t, :], acc[0:r, t, :])
            link(ins)
            for t in range(NT):
                r = ROWS[t]
                ins = V.bn_aggr(mv[0:r, t, :], stats[0:r, t, :])
            link(ins)
            V.tensor_scalar(rs[:, 0, :], mv[:, :, 1], 1e-5, None, ALU.add).then_inc(S["bn_done"], 1)
            dve.wait_ge(S["sqrt_done"], 1)
            link(V.reciprocal(rs[:, 2, :], rs[:, 1, :]))
            link(V.tensor_tensor(rs[:, 3, :], rs[:, 2, :], rs[:, 2, :], ALU.mult))
            link(V.tensor_tensor(rs[:, 3, :], rs[:, 3, :], rs[:, 0, :], ALU.mult))
            link(V.tensor_scalar(rs[:, 3, :], rs[:, 3, :], -0.5, 1.5, ALU.mult, ALU.add))
            link(V.tensor_tensor(rs[:, 2, :], rs[:, 2, :], rs[:, 3, :], ALU.mult))

            def normalize(t):
                r = ROWS[t]
                if t >= 2:
                    dve.wait_ge(S["hT_ps"], t - 1)
                    dve.wait_ge(S["h16lo_ready"], t - 1)
                    dve.wait_ge(S["h16hi_ready"], t - 1)
                V.tensor_scalar(h32[0:r, t % 2, :], acc[0:r, t, :], mv[0:r, t, 0:1], rs[0:r, 2, t:t + 1],
                                ALU.subtract, ALU.mult).then_inc(S["xn_ready"], 1)

            def low_parts(t):
                r = ROWS[t]
                dve.wait_ge(S["h16hi_ready"], t + 1)
                V.scalar_tensor_tensor(out=y[0:r, 1, t, :], in0=h32[0:r, t % 2, :], scalar=HSCALE,
                                       in1=y[0:r, 0, t, :], op0=ALU.mult, op1=ALU.subtract
                                       ).then_inc(S["h16lo_ready"], 1)
                dve.wait_ge(S["hThi_ready"], t + 1)
                V.scalar_tensor_tensor(out=hT[:, 1, :, t * P:t * P + r], in0=hT32[:, :, t * P:t * P + r],
                                       scalar=HSCALE, in1=hT[:, 0, :, t * P:t * P + r],
                                       op0=ALU.mult, op1=ALU.subtract).then_inc(S["hTlo_ready"], 1)

            normalize(0)
            normalize(1)
            for t in range(NT):
                low_parts(t)
                if t + 2 < NT:
                    normalize(t + 2)

            dve.wait_ge(S["b0_ps"], 1)
            link(V.tensor_copy(b0T[:], ps_a[1][:, 0:E * FC]))
            V.tensor_reduce(bmax[:], b0T[:].rearrange("p (e c) -> p e c", c=FC), AX.X, ALU.max,
                            apply_absolute_value=True).then_inc(S["bmax_ready"], 1)

            dve.wait_ge(S["gates_ps"], 1)
            pg = ps_a[0][:, 0:NT * E].rearrange("p (t e) -> p t e", e=E)
            V.tensor_copy(logit[:, 0:NT - 1, :], pg[:, 0:NT - 1, :])
            link(V.tensor_copy(logit[0:TAIL, NT - 1, :], pg[0:TAIL, NT - 1, :]))
            link(V.tensor_tensor(logit[:], logit[:], gb[:].rearrange("p (o e) -> p o e", o=1
                                                                     ).to_broadcast([P, NT, E]), ALU.add))
            link(V.memset(wins[:], 0.0))
            for i in range(E):
                for j in range(i + 1, E):
                    link(V.tensor_tensor(beat[:, 0, :], logit[:, :, i], logit[:, :, j], ALU.is_ge))
                    V.tensor_tensor(wins[:, :, i], wins[:, :, i], beat[:, 0, :], ALU.add)
                    link(V.tensor_scalar(beat[:, 1, :], beat[:, 0, :], -1.0, 1.0, ALU.mult, ALU.add))
                    link(V.tensor_tensor(wins[:, :, j], wins[:, :, j], beat[:, 1, :], ALU.add))
            link(V.tensor_reduce(gmax[:, :, 0], logit[:], AX.X, ALU.max))
            V.tensor_tensor(logit[:], logit[:], gmax[:].to_broadcast([P, NT, E]), ALU.subtract
                            ).then_inc(S["gates_done"], 1)
            link(V.tensor_scalar(wins[:], wins[:], float(E - 2), None, ALU.is_ge))
            dve.wait_ge(S["exp_done"], 1)
            link(V.tensor_reduce(gsum[:, :, 0], logit[:], AX.X, ALU.add))
            link(V.reciprocal(gsum[:], gsum[:]))
            link(V.tensor_tensor(logit[:], logit[:], gsum[:].to_broadcast([P, NT, E]), ALU.mult))
            link(V.tensor_tensor(gate[:].rearrange("p e t -> p t e"), logit[:], wins[:], ALU.mult))

            dve.wait_ge(S["C_zero"], 1)
            need_slow = dve.value_load(flag_i[:], min_val=0, max_val=1)

            def one_hots(u, gi, cols):
                for c in range(CH):
                    V.tensor_scalar(hotA[:, u, c, :], iota16[0:EP, :], cols[:, c, bass.ds(gi, 1)], None,
                                    ALU.is_equal)
                    ins = V.tensor_scalar(hotB[:, u, c, :], iota16[0:EP, 0:P], slo_c[:, c, bass.ds(gi, 1)],
                                          None, ALU.is_equal)
                return ins

            def add_counts(u, gi, b):
                dve.wait_ge(S["counted"], gi + 1)
                dve.wait_ge(S["added"], CREDIT + gi)
                dest = C3[:, :, bass.ds(b, WIN)]
                V.tensor_tensor(dest, ring[u][:, 0:AW].rearrange("p (t n) -> p t n", n=WIN), dest, ALU.add
                                ).then_inc(S["added"], 1)

            def load_base(gi):
                return dve.value_load(base_i[0:1, bass.ds(gi, 1)], min_val=0, max_val=N - 1)

            with dve.If(need_slow == 0):
                one_hots(0, 0, col_c).then_inc(S["hot_ready"], 1)
                with dve.Fori(0, G // SLOTS - 1) as i:
                    for u in range(SLOTS):
                        one_hots((u + 1) % SLOTS, i * SLOTS + u + 1, col_c).then_inc(S["hot_ready"], 1)
                        add_counts(u, i * SLOTS + u, load_base(i * SLOTS + u))
                for u in range(SLOTS):
                    g = G - SLOTS + u
                    if u + 1 < SLOTS:
                        one_hots(u + 1, g + 1, col_c).then_inc(S["hot_ready"], 1)
                    add_counts(u, g, load_base(g))
                dve.wait_ge(S["added"], CREDIT + G)
            with dve.Else():
                with dve.Fori(0, NWIN) as w:
                    slow_columns(dve, V, w)
                    V.memset(done_mark[:, 1:2], 0.0)
                    with dve.Fori(0, G) as g:
                        one_hots(0, g, col_c).then_inc(S["slow_hot"], 1)
                        dve.wait_ge(S["slow_counted"], w * G + g + 1)
                    pw = ring[0][:, 0:AW].rearrange("p (t n) -> p t n", n=WIN)
                    V.tensor_copy(near16, pw).then_inc(S["slow_evac"], 1)
                    dve.wait_ge(S["slow_evac"], w * 6 + 5)
                    V.tensor_copy(C3[:, :, bass.ds(w * WIN, WIN)], near16)
                    V.tensor_tensor(rest8, pw, near16, ALU.subtract, saturate=False).then_inc(S["slow_evac"], 1)
                    dve.wait_ge(S["slow_evac"], w * 6 + 6)
                    V.tensor_copy(R3[:, :, bass.ds(w * WIN, WIN)].bitcast(U8), rest8.bitcast(U8)
                                  ).then_inc(S["slow_read"], 1)
                dve.wait_ge(S["slow_read"], CREDIT + NWIN)
            V.memset(done_mark[:, 0:1], 0.0).then_inc(S["C_ready"], 1)

            dve.wait_ge(S["deg_ps"], 1)
            for k, (n0, w) in enumerate(NC):
                link(V.tensor_scalar(inv_bc[:, n0:n0 + w], ring[k][:, 0:w], 1.0, None, ALU.max))
                link(V.reciprocal(inv_bc[:, n0:n0 + w], inv_bc[:, n0:n0 + w]))
                ins = V.scalar_tensor_tensor(out=inv_bc[:, n0:n0 + w], in0=ring[k][:, 0:w], scalar=0.0,
                                             in1=inv_bc[:, n0:n0 + w], op0=ALU.is_gt, op1=ALU.mult)
            ins.then_inc(S["inv_ready"], 1)
            dve.wait_ge(S["inv_ready"], 1)

            def w_max(q):
                dve.wait_ge(S["w_in"], (q + 1) * 32)
                V.tensor_reduce(wmax[:], w32_flat, AX.X, ALU.max, apply_absolute_value=True
                                ).then_inc(S["wmax_ready"], 1)
                dve.wait_ge(S["wmax_all"], q + 1)

            sci = sc.ap().bitcast(I32)
            SC_OPS = [0]

            def scales(q, e, layer, steps):
                s0 = 3 * layer

                def then(ins):
                    steps(ins)
                then(V.tensor_scalar(sc[:, s0 + 2:s0 + 3], wmaxA[:], TINY, None, ALU.max))
                then(V.tensor_scalar(sci[:, s0 + 1:s0 + 2], sci[:, s0 + 2:s0 + 3], 0x7F800000, None,
                                     ALU.bitwise_and))
                then(V.tensor_scalar(sci[:, s0:s0 + 1], sci[:, s0 + 1:s0 + 2], -1.0, float(268 * EXP1),
                                     ALU.mult, ALU.add))
                then(V.tensor_scalar(sci[:, s0 + 1:s0 + 2], sci[:, s0 + 1:s0 + 2], float(-14 * EXP1), None,
                                     ALU.add))
                if layer == 0:
                    then(V.scalar_tensor_tensor(out=sc[:, 9:10], in0=sc[:, 2:3], scalar=2.0 * D,
                                                in1=bmaxA[:, bass.ds(e, 1)], op0=ALU.mult, op1=ALU.add))
                    then(V.tensor_scalar(sci[:, 8:9], sci[:, 9:10], 0x7F800000, None, ALU.bitwise_and))
                    then(V.tensor_scalar(sci[:, 7:8], sci[:, 8:9], -1.0, float(268 * EXP1), ALU.mult, ALU.add))
                    then(V.tensor_scalar(sci[:, 8:9], sci[:, 8:9], float(-14 * EXP1), None, ALU.add))
                    then(V.scalar_tensor_tensor(out=sc[:, 10:11], in0=sc[:, 1:2], scalar=1.0 / HSCALE,
                                                in1=sc[:, 7:8], op0=ALU.mult, op1=ALU.mult))

            def w_low(layer):
                return V.scalar_tensor_tensor(
                    out=W16[:, layer, 1, :, :, :].rearrange("p a c d -> p (a c d)"), in0=w32_flat,
                    scalar=sc[:, 3 * layer:3 * layer + 1],
                    in1=W16[:, layer, 0, :, :, :].rearrange("p a c d -> p (a c d)"),
                    op0=ALU.mult, op1=ALU.subtract)

            dve.wait_ge(S["bmax_all"], 1)
            dve.wait_ge(S["consts_in"], 16 * (2 + E))
            w_max(0)
            scales(0, 0, 0, link)
            V.memset(done_mark[:, 0:1], 0.0).then_inc(S["scale_ready"], 1)
            dve.wait_ge(S["invcol_ps"], 1)
            V.tensor_copy(inv_col[:, 0:NT - 1], ps_a[0][:, 0:NT - 1])
            V.tensor_copy(inv_col[0:TAIL, NT - 1:NT], ps_a[0][0:TAIL, NT - 1:NT]).then_inc(S["invcol_ready"], 1)

            def agg0_low(i):
                c, (n0, w) = i // len(NC), NC[i % len(NC)]
                dve.wait_ge(S["agg0_hi"], i + 1)
                V.tensor_tensor(aT[:, 1, c, n0:n0 + w], tmp32[:, i % 2, 0:w], aT[:, 0, c, n0:n0 + w],
                                ALU.subtract).then_inc(S["agg0_lo"], 1)

            for i in range(L0):
                c, (n0, w) = i // len(NC), NC[i % len(NC)]
                dve.wait_ge(S["ring_full"], i + 1)
                if i >= 2:
                    dve.wait_ge(S["agg0_lo"], i - 1)
                V.tensor_tensor(tmp32[:, i % 2, 0:w], ring[i % SLOTS][:, 0:w], inv_bc[:, n0:n0 + w], ALU.mult
                                ).then_inc(S["agg0_scaled"], 1)
                if i >= 1:
                    agg0_low(i - 1)
                if i == 2:
                    dve.wait_ge(S["Whi_ready"], 1)
                    w_low(0).then_inc(S["Wlo_ready"], 1)
            agg0_low(L0 - 1)
            V.memset(done_mark[:, 0:1], 0.0).then_inc(S["l0_lo"], L0)

            base = chain[0]
            PER = 1 + 4 + 1 + 9

            def expert(e, last):
                cnt = [0]

                def step(ins):
                    cnt[0] += 1
                    ins.then_inc(S["dve"], 1)
                    dve.wait_ge(S["dve"], e * PER + base + cnt[0])

                V.tensor_copy(gate_now[:], gate[:, bass.ds(e, 1), :].rearrange("p o t -> p (o t)"))
                V.tensor_copy(sc[:, 11:12], sc[:, 8:9])
                V.tensor_copy(sc[:, 6:7], sc[:, 10:11])
                step(V.tensor_scalar(bs[:], b0T[:, bass.ds(e * FC, FC)], sc[:, 7:8], None, ALU.mult))
                V.memset(done_mark[:, 0:1], 0.0).then_inc(S["h1_scale_ready"], 1)
                for i in range(L0):
                    c, (n0, w) = i // len(NC), NC[i % len(NC)]
                    dve.wait_ge(S["l0_read"], e * L0 + i + 1)
                    V.tensor_tensor(h1T[:, 1, c, n0:n0 + w], tmp32[:, i % 2, 0:w], h1T[:, 0, c, n0:n0 + w],
                                    ALU.subtract).then_inc(S["l0_lo"], 1)
                    if i == 0:
                        w_max(e * 2 + 1)
                        scales(e * 2 + 1, e, 1, step)
                        step(V.tensor_tensor(sc[:, 5:6], sc[:, 4:5], sc[:, 11:12], ALU.mult))
                        V.tensor_scalar(inv_s[:], inv_col[:], sc[:, 5:6], 1.0 / YSCALE, ALU.mult, ALU.mult)
                        V.memset(done_mark[:, 0:1], 0.0).then_inc(S["scale_ready"], 1)
                    if i == 3:
                        dve.wait_ge(S["Whi_ready"], e * 2 + 2)
                        w_low(1).then_inc(S["Wlo_ready"], 1)
                for t in range(NT):
                    i, r = L0 + t, ROWS[t]
                    dve.wait_ge(S["y_hi"], e * NT + t + 1)
                    V.scalar_tensor_tensor(out=y[0:r, 1, t, :], in0=ring[i % SLOTS][0:r, :], scalar=YSCALE,
                                           in1=y[0:r, 0, t, :], op0=ALU.mult, op1=ALU.subtract
                                           ).then_inc(S["y_lo"], 1)
                dve.wait_ge(S["b1_in"], 16 * e + 16)

                def add_tile(t):
                    r = ROWS[t]
                    dve.wait_ge(S["relu_ready"], e * NT + t + 1)
                    V.tensor_tensor(acc[0:r, t, :], acc[0:r, t, :], zt[0:r, t % 3, :], ALU.add
                                    ).then_inc(S["tile_done"], 1)

                for t in range(NT):
                    r = ROWS[t]
                    dve.wait_ge(S["z_full"], e * NT + t + 1)
                    dve.wait_ge(S["tile_done"], CREDIT + e * NT + max(t - 2, 0))
                    V.scalar_tensor_tensor(out=zt[0:r, t % 3, :], in0=ps_z[t % 2][0:r, :],
                                           scalar=sc[0:r, 5:6], in1=bias1[0:r, :], op0=ALU.mult, op1=ALU.add
                                           ).then_inc(S["z_read"], 1)
                    dve.wait_ge(S["z_read"], CREDIT + e * NT + t + 1)
                    dve.wait_ge(S["a_full"], e * NT + t + 1)
                    V.scalar_tensor_tensor(out=zt[0:r, t % 3, :], in0=ps_a[t % 2][0:r, :],
                                           scalar=inv_s[0:r, t:t + 1], in1=zt[0:r, t % 3, :],
                                           op0=ALU.mult, op1=ALU.add).then_inc(S["t_ready"], 1)
                    if t >= 1:
                        add_tile(t - 1)
                    if t == 1 and not last:
                        w_max(e * 2 + 2)
                        scales(e * 2 + 2, e + 1, 0, step)
                        V.memset(done_mark[:, 0:1], 0.0).then_inc(S["scale_ready"], 1)
                    if t == 4 and not last:
                        dve.wait_ge(S["Whi_ready"], e * 2 + 3)
                        w_low(0).then_inc(S["Wlo_ready"], 1)
                add_tile(NT - 1)
                assert last or cnt[0] == PER

            with dve.Fori(0, E - 1) as e:
                expert(e, False)
            expert(E - 1, True)

        @block.tensor
        def _(pe):
            T = nc.tensor
            pe.wait_ge(S["ident_ready"], 2)
            pe.wait_ge(S["edges_split"], 1)
            for k, v in enumerate((dst_f, shi_f, slo_f)):
                for c in range(CH):
                    T.transpose(ring[k][0:EP, c * G:(c + 1) * G], v[:, c * EP:(c + 1) * EP], ident[0:G, 0:G])
            T.transpose(ring[3][0:EP, 0:G], mm_bc[:, 0, :], ident[0:G, 0:G])
            T.transpose(ring[3][0:EP, G:2 * G], mm_bc[:, 1, :], ident[0:G, 0:G]).then_inc(S["edges_T"], 1)

            pe.wait_ge(S["consts_in"], 16 * (2 + E))
            T.transpose(ps_a[1][:, 0:E * FC], b_rows[:], ident[0:E * FC, 0:E * FC]).then_inc(S["b0_ps"], 1)

            def gates(t):
                r = ROWS[t]
                pe.wait_ge(S["hT32_ready"], t + 1)
                for c in range(FC):
                    mm = T.matmul(ps_a[0][0:r, t * E:(t + 1) * E], hT32[:, c, t * P:t * P + r], gW[:, c, :],
                                  start=(c == 0), stop=(c == FC - 1))
                return mm

            for t in range(NT):
                r = ROWS[t]
                pe.wait_ge(S["h32_ready"], t + 1)
                if t >= 2:
                    pe.wait_ge(S["hThi_ready"], t - 1)
                for c in range(FC):
                    mm = T.transpose(ps_z[t % 2][:, c * P:c * P + r], h32[0:r, t % 2, c * P:(c + 1) * P],
                                     ident[0:r, 0:r])
                mm.then_inc(S["hT_ps"], 1)
                if t >= 1:
                    gates(t - 1)
            gates(NT - 1).then_inc(S["gates_ps"], 1)

            pe.wait_ge(S["flag_ready"], 1)
            need_slow = pe.value_load(flag_i[:], min_val=0, max_val=1)

            def count(u, start, stop):
                for c in range(CH):
                    mm = T.matmul(ring[u][:, 0:AW], hotB[:, u, c, :], hotA[:, u, c, :],
                                  start=(start and c == 0), stop=(stop and c == CH - 1))
                return mm

            with pe.If(need_slow == 0):
                for g in range(SLOTS):
                    pe.wait_ge(S["hot_ready"], g + 1)
                    count(g, True, True).then_inc(S["counted"], 1)
                with pe.Fori(1, G // SLOTS) as i:
                    for u in range(SLOTS):
                        pe.wait_ge(S["hot_ready"], i * SLOTS + u + 1)
                        pe.wait_ge(S["added"], CREDIT + i * SLOTS + u - (SLOTS - 1))
                        count(u, True, True).then_inc(S["counted"], 1)
            with pe.Else():
                with pe.Fori(0, NWIN) as w:
                    pe.wait_ge(S["slow_read"], CREDIT + w)
                    pe.wait_ge(S["slow_hot"], w * G + 1)
                    count(0, True, False).then_inc(S["slow_counted"], 1)
                    with pe.Fori(1, G - 1) as g:
                        pe.wait_ge(S["slow_hot"], w * G + g + 1)
                        count(0, False, False).then_inc(S["slow_counted"], 1)
                    pe.wait_ge(S["slow_hot"], (w + 1) * G)
                    count(0, False, True).then_inc(S["slow_counted"], 1)

            pe.wait_ge(S["C_ready"], 1)
            pe.wait_ge(S["ones_ready"], 1)
            for k, (n0, w) in enumerate(NC):
                T.matmul(ring[k][:, 0:w], ones16[:], C3[:, 0, n0:n0 + w], start=True, stop=False)
                with pe.If(need_slow != 0):
                    for t in range(NT):
                        T.matmul(ring[k][:, 0:w], ones16[0:ROWS[t], :], R3[0:ROWS[t], t, n0:n0 + w],
                                 start=False, stop=False)
                for t in range(1, NT):
                    mm = T.matmul(ring[k][:, 0:w], ones16[0:ROWS[t], :], C3[0:ROWS[t], t, n0:n0 + w],
                                  start=False, stop=(t == NT - 1))
            mm.then_inc(S["deg_ps"], 1)
            pe.wait_ge(S["inv_ready"], 1)
            for t in range(NT):
                mm = T.matmul(ps_a[0][0:ROWS[t], t:t + 1], inv_bc[0:1, t * P:t * P + ROWS[t]], ident[0:1, 0:1],
                              start=True, stop=True)
            mm.then_inc(S["invcol_ps"], 1)

            pe.wait_ge(S["h16lo_ready"], NT)
            for i in range(L0):
                c, (n0, w) = i // len(NC), NC[i % len(NC)]
                if i >= SLOTS:
                    pe.wait_ge(S["agg0_scaled"], i - SLOTS + 1)

                def part(k, t, M3, start, stop):
                    r = ROWS[t]
                    return T.matmul(ring[i % SLOTS][:, 0:w], y[0:r, k, t, c * P:(c + 1) * P],
                                    M3[0:r, t, n0:n0 + w], start=start, stop=stop)

                part(0, 0, C3, True, False)
                with pe.If(need_slow != 0):
                    for t in range(NT):
                        part(0, t, R3, False, False)
                        part(1, t, R3, False, False)
                part(1, 0, C3, False, False)
                for t in range(1, NT):
                    part(0, t, C3, False, False)
                    mm = part(1, t, C3, False, t == NT - 1)
                mm.then_inc(S["ring_full"], 1)

            PAIRS = ((0, 0), (0, 1), (1, 0))

            def expert(e, last):
                pe.wait_ge(S["Wlo_ready"], e * 2 + 1)
                pe.wait_ge(S["hTlo_ready"], NT)
                pe.wait_ge(S["y_lo"], CREDIT + e * NT)
                pe.wait_ge(S["agg0_lo"], L0)
                for i in range(L0):
                    c, (n0, w) = i // len(NC), NC[i % len(NC)]
                    if i >= SLOTS:
                        pe.wait_ge(S["l0_read"], e * L0 + i - SLOTS + 1)
                    n = 0
                    for m, X in ((1, hT), (0, aT)):
                        for k in range(FC):
                            for a, b in PAIRS:
                                mm = T.matmul(ring[i % SLOTS][:, 0:w], W16[:, 0, a, m, k, c * P:(c + 1) * P],
                                              X[:, b, k, n0:n0 + w], start=(n == 0), stop=(n == 6 * FC - 1))
                                n += 1
                    mm.then_inc(S["ring_full"], 1)
                pe.wait_ge(S["Wlo_ready"], e * 2 + 2)
                for t in range(NT):
                    i, r = L0 + t, ROWS[t]
                    if t == 0:
                        pe.wait_ge(S["l0_lo"], e * L0 + 2 * L0)
                    if t < SLOTS:
                        pe.wait_ge(S["l0_read"], e * L0 + i - SLOTS + 1)
                    else:
                        pe.wait_ge(S["y_lo"], CREDIT + e * NT + t - SLOTS + 1)
                    n = 0
                    for k in range(FC):
                        for a, b in PAIRS:
                            mm = T.matmul(ring[i % SLOTS][0:r, :], h1T[:, b, k, t * P:t * P + r],
                                          W16[:, 1, a, 0, k, :], start=(n == 0), stop=(n == 3 * FC - 1))
                            n += 1
                    mm.then_inc(S["ring_full"], 1)
                for t in range(NT):
                    r = ROWS[t]
                    if t < 2:
                        pe.wait_ge(S["t_ready"], CREDIT + e * NT)
                    else:
                        pe.wait_ge(S["z_read"], CREDIT + e * NT + t - 1)
                    n = 0
                    for k in range(FC):
                        for a, b in PAIRS:
                            mm = T.matmul(ps_z[t % 2][0:r, :], h1T[:, b, k, t * P:t * P + r],
                                          W16[:, 1, a, 1, k, :], start=(n == 0), stop=(n == 3 * FC - 1))
                            n += 1
                    mm.then_inc(S["z_full"], 1)
                    if t == 0:
                        pe.wait_ge(S["y_lo"], CREDIT + (e + 1) * NT)
                    if t >= 2:
                        pe.wait_ge(S["t_ready"], CREDIT + e * NT + t - 1)

                    def part(k, s, M3, start, stop):
                        q = ROWS[s]
                        return T.matmul(ps_a[t % 2][0:r, :], M3[0:q, s, t * P:t * P + r], y[0:q, k, s, :],
                                        start=start, stop=stop)

                    part(0, 0, C3, True, False)
                    with pe.If(need_slow != 0):
                        for s in range(NT):
                            part(0, s, R3, False, False)
                            part(1, s, R3, False, False)
                    part(1, 0, C3, False, False)
                    for s in range(1, NT):
                        part(0, s, C3, False, False)
                        mm = part(1, s, C3, False, s == NT - 1)
                    mm.then_inc(S["a_full"], 1)

            with pe.Fori(0, E - 1) as e:
                expert(e, False)
            expert(E - 1, True)


_INS = ["x", "src", "dst", "L0_gnn_gate_W", "L0_gnn_gate_b", "L0_gnn_Wl", "L0_gnn_bl", "L0_gnn_Wr"]
_OUTS = [((1250, 512), "float32")]


def kernel(**inputs):
    import numpy as _np
    import concourse.bacc as _bacc
    from concourse import mybir as _mybir
    from concourse.bass_utils import run_bass_kernel_spmd as _run

    nc = _bacc.Bacc("TRN2", target_bir_lowering=False, num_devices=1)
    arrays, args = {}, []
    for name in _INS:
        a = _np.ascontiguousarray(inputs[name])
        arrays[f"in_{name}_dram"] = a
        args.append(nc.dram_tensor(f"in_{name}_dram", a.shape, _mybir.dt.from_np(a.dtype), kind="ExternalInput").ap())
    for i, (shape, dtype) in enumerate(_OUTS):
        dt = _mybir.dt.from_np(_np.dtype(dtype))
        args.append(nc.dram_tensor(f"out_{i}_dram", shape, dt, kind="ExternalOutput").ap())
    sage_moe_kernel(nc, *args)
    r = _run(nc, [arrays], core_ids=[0])
    return r.results[0]["out_0_dram"]
```

```python
from contextlib import ExitStack

import concourse.bass as bass
from concourse import mybir

ALU = mybir.AluOpType
ACT = mybir.ActivationFunctionType
AX = mybir.AxisListType
F32 = mybir.dt.float32
F16 = mybir.dt.float16
F8 = mybir.dt.float8e4
I32 = mybir.dt.int32
U8 = mybir.dt.uint8

P = 128
WIN = 48
CREDIT = 1
ACT_B = 4
SLOTS = 4
HSCALE = 1024.0
YSCALE = 2.0 ** -24
EXP1 = 1 << 23
TINY = 2.0 ** -60


def sage_moe_kernel(nc, x, src, dst, gate_W, gate_b, Wl, bl, Wr, out):
    N, D = x.shape
    E, L = Wl.shape[0], Wl.shape[1]
    NE = src.shape[0]
    FC = D // P
    NT = (N + P - 1) // P
    ROWS = [min(P, N - t * P) for t in range(NT)]
    TAIL = ROWS[-1]
    CH = 5
    EP = 125
    EG = CH * EP
    G = NE // EG
    assert G * EG == NE and G == 64 and G % SLOTS == 0
    AW = NT * WIN
    assert AW <= 512
    NWIN = (N + WIN - 1) // WIN
    CW = 1300
    assert CW >= N - 1 + WIN and CW >= NWIN * WIN
    NC = [(0, 417), (417, 417), (834, 416)]
    NCW = 417
    L0 = FC * len(NC)
    RING = L0 + NT
    assert RING - SLOTS >= L0 and L0 % 2 == 0 and NT % 2 == 0

    with ExitStack() as ctx:
        def sb(name, shape, dt):
            return ctx.enter_context(nc.sbuf_tensor(name, shape, dt))

        def psum(name, shape, dt=F32):
            return ctx.enter_context(nc.psum_tensor(name, shape, dt))

        def sem(name):
            return ctx.enter_context(nc.semaphore(name))

        ring = [psum(f"ring{i}", [P, 512]) for i in range(SLOTS)]
        ps_z = [psum(f"ps_z{i}", [P, 512]) for i in range(2)]
        ps_a = [psum(f"ps_a{i}", [P, 512]) for i in range(2)]

        C = sb("C", [P, NT * CW], F16)
        C_rest = sb("C_rest", [P, NT * CW], F8)
        hT = sb("hT", [P, 2, FC, N], F16)
        aT = sb("aT", [P, 2, FC, N], F16)
        h1T = sb("h1T", [P, 2, FC, N], F16)
        W16a = sb("W16a", [P, 2, FC, D], F16)
        W16b = sb("W16b", [P, 2, 2, FC, D], F16)
        Wb16 = sb("Wb16", [P, 2, 2, FC, P], F16)
        wrA = sb("wrA", [P, E * FC], F32)
        ones32 = sb("ones32", [P, 1], F32)
        wbmax = sb("wbmax", [P, 2], F32)
        bsc = sb("bsc", [P, 2, 4], F32)
        hbound = sb("hbound", [P, E], F32)
        nslo_c = sb("nslo_c", [EP, CH, G], F32)
        W32 = sb("W32", [P, 2, FC * D], F32)
        acc = sb("acc", [P, NT, D], F32)
        y = sb("y", [P, 2, NT, D], F16)
        tmp32 = sb("tmp32", [P, len(NC), NCW], F32)
        inv_bc = sb("inv_bc", [P, N], F32)
        bias1 = sb("bias1", [P, D], F32)
        zt = sb("zt", [P, 3, D], F32)
        ident = sb("ident", [P, P], F32)
        ones16 = sb("ones16", [P, P], F16)
        iota_i = zt.ap().rearrange("p a d -> p (a d)")[:, 0:AW].bitcast(I32)
        iota16 = sb("iota16", [P, AW], F16)
        minmax = sb("minmax", [G, 2], F32)
        dst_c, shi_c, slo_c = (inv_bc[0:EP, k * CH * G:(k + 1) * CH * G].rearrange("p (c g) -> p c g", c=CH)
                               for k in range(3))
        col_c = sb("col_c", [EP, CH, G], F32)
        row = sb("row", [P, 2, G], F32)
        base_i = sb("base_i", [1, G], I32)
        chk = sb("chk", [1, 3, G], F32)
        chk3 = sb("chk3", [1, 8], F32)
        flag_i = sb("flag_i", [1, 1], I32)
        stats = sb("stats", [P, NT, 6], F32)
        mv = sb("mv", [P, NT, 2], F32)
        rs = sb("rs", [P, 4, NT], F32)
        gW = sb("gW", [P, FC, E], F32)
        gb = sb("gb", [P, E], F32)
        logit = sb("logit", [P, NT, E], F32)
        wins = sb("wins", [P, NT, E], F32)
        beat = sb("beat", [P, 2, NT], F32)
        gmax = sb("gmax", [P, NT, 1], F32)
        gsum = sb("gsum", [P, NT, 1], F32)
        gate = sb("gate", [P, E, NT], F32)
        gate_now = sb("gate_now", [P, NT], F32)
        inv_col = sb("inv_col", [P, NT], F32)
        inv_s = sb("inv_s", [P, NT], F32)
        b_rows = sb("b_rows", [E * FC, P], F32)
        b0T = sb("b0T", [P, E * FC], F32)
        bmax = sb("bmax", [P, E], F32)
        bmaxA = sb("bmaxA", [P, E], F32)
        bs = sb("bs", [P, FC], F32)
        wmax = sb("wmax", [P, 1], F32)
        wmaxA = sb("wmaxA", [P, 1], F32)
        sc = sb("sc", [P, 16], F32)
        done_mark = sb("done_mark", [1, 16], F32)

        hotA = aT.ap().rearrange("p a c n -> p (a c n)")[0:EP, 0:SLOTS * CH * AW].rearrange(
            "p (u c a) -> p u c a", u=SLOTS, c=CH)
        hotB = W16b.ap().rearrange("p a b c d -> p (a b c d)")[0:EP, 0:SLOTS * CH * P].rearrange(
            "p (u c b) -> p u c b", u=SLOTS, c=CH)
        Wst = W32.ap()[:, 1, 0:2 * FC * P].rearrange("p (s w) -> p s w", s=2)
        w32_flat = W32.ap().rearrange("p a b -> p (a b)")

        def edge_tmp(k):
            return w32_flat[0:G, k * EG:(k + 1) * EG]

        dst_i, src_i, dst_f, shi_f, slo_f = (edge_tmp(k) for k in range(5))
        shi_i = edge_tmp(5)
        mm_bc = w32_flat[0:G, 6 * EG:6 * EG + 2 * EP].rearrange("p (k e) -> p k e", k=2)
        hT32 = h1T.ap().rearrange("p a c n -> p (a c n)").bitcast(F32).rearrange("p (c n) -> p c n", c=FC)
        h32 = zt
        absB = zt.ap()[0:EP, 0, 0:ACT_B * P].bitcast(F16).rearrange("p (s c b) -> p s c b", s=2, c=ACT_B)
        near16 = zt.ap()[:, 1, 0:AW // 2].bitcast(F16).rearrange("p (t n) -> p t n", n=WIN)
        rest8 = zt.ap()[:, 2, 0:AW // 4].bitcast(F8).rearrange("p (t n) -> p t n", n=WIN)
        R_dram = nc.dram_tensor("R_dram", [E, FC, len(NC), P, NCW], F32, kind="Internal").ap()
        C3 = C.ap().rearrange("p (t n) -> p t n", t=NT)
        R3 = C_rest.ap().rearrange("p (t n) -> p t n", t=NT)

        names = ("dst_in src_in consts_in w_in b1_in out_done edges_split edges_T win_ready"
                 " ident_ready iota_ready iotas_cast C_zero ones_ready flag_ready dve"
                 " bn_done sqrt_done h1_scale_ready xn_ready h32_ready h16hi_ready h16lo_ready hT_ps hT32_ready hThi_ready hTlo_ready"
                 " gates_ps b0_ps b0_ready exp_done gates_done"
                 " hot_ready counted added slow_hot slow_counted slow_read slow_evac C_ready"
                 " deg_ps inv_ready invcol_ps invcol_ready"
                 " ring_full agg0_scaled agg0_hi agg0_lo"
                 " wmax_ready wmax_all scale_ready Whi_ready Wlo_ready"
                 " l0_sum l0_hi l0_out l0_lo wbmax_ready wbmax_all wb_scale wb_hi wb_lo wchain r_full r_evac hotB_ready nslo_ready absB_ready logits_read y_hi y_lo z_full a_full z_read t_ready relu_ready tile_done bmax_ready bmax_all").split()
        S = {n: sem(n) for n in names}
        wst_in = [sem(f"wst_in{k}") for k in range(2)]
        r_stored = [sem(f"r_stored{k}") for k in range(len(NC))]
        r_in = [sem(f"r_in{k}") for k in range(len(NC))]
        NB = E * FC
        x_in = [sem(f"x_in{j}") for j in range(NT // 2)]

        x_rows = x.rearrange("(o n) d -> o n d", o=1)
        Wl_q = Wl.rearrange("e l (c p) d -> (e l) p c d", p=P)
        Wr_q = Wr.rearrange("e l (c p) d -> (e l) p c d", p=P)
        W32v = W32.ap().rearrange("p a (c d) -> p a c d", c=FC)
        QN = E * L

        ps_r = (ps_z[0], ps_z[1], ps_a[0])

        block = ctx.enter_context(nc.Block())

        @block.sync
        def _(sp):
            sp.dma_start(dst_i.bitcast(I32), dst.rearrange("(g e) -> g e", e=EG)).then_inc(S["dst_in"], 16)
            sp.dma_start(src_i.bitcast(I32), src.rearrange("(g e) -> g e", e=EG)).then_inc(S["src_in"], 16)
            for j in range(NT // 2):
                t = 2 * j
                if ROWS[t + 1] == P:
                    sp.dma_start(acc[:, t:t + 2, :], x[t * P:(t + 2) * P, :].rearrange("(a p) d -> p a d", p=P)
                                 ).then_inc(x_in[j], 16)
                else:
                    sp.dma_start(acc[:, t, :], x[t * P:(t + 1) * P, :]).then_inc(x_in[j], 16)
                    sp.dma_start(acc[0:TAIL, t + 1, :], x[(t + 1) * P:N, :]).then_inc(x_in[j], 16)
            sp.dma_start(gW[:], gate_W.rearrange("(c p) e -> p c e", p=P)).then_inc(S["consts_in"], 16)
            sp.dma_start(gb[:], gate_b.partition_broadcast(P)).then_inc(S["consts_in"], 16)
            for e in range(E):
                sp.dma_start(b_rows[e * FC:(e + 1) * FC, :], bl[e, 0, :].rearrange("(c p) -> c p", p=P)
                             ).then_inc(S["consts_in"], 16)

            def load_block(b):
                e, c = b // FC, b % FC
                if b >= 2:
                    sp.wait_ge(S["wb_lo"], b - 1)
                sp.dma_start(Wst[:, b % 2, :].rearrange("p (c m) -> p c m", c=FC),
                             Wr[e, 0, :, c * P:(c + 1) * P].rearrange("(c p) m -> p c m", p=P)
                             ).then_inc(wst_in[b % 2], 16)

            sp.wait_ge(S["edges_T"], 1)
            load_block(0)
            load_block(1)
            for b in range(NB):
                for k, (n0, w) in enumerate(NC):
                    sp.wait_ge(S["r_evac"], len(NC) + b * len(NC) + k + 1)
                    sp.dma_start(R_dram[b // FC, b % FC, k, :, 0:w], tmp32[:, k, 0:w]).then_inc(r_stored[k], 16)
                if b + 2 < NB:
                    load_block(b + 2)
            for k in range(len(NC)):
                sp.wait_ge(r_stored[k], 16 * (NB + 1))

            with sp.Fori(0, E) as e:
                for i in range(L0):
                    c, k, w = i // len(NC), i % len(NC), NC[i % len(NC)][1]
                    if i == 0:
                        sp.wait_ge(S["tile_done"], CREDIT + e * NT)
                        sp.dma_start(bias1[:], bl[bass.ds(e, 1), 1, :].rearrange("a d -> (a d)"
                                                                                 ).partition_broadcast(P)
                                     ).then_inc(S["b1_in"], 16)
                    if i >= len(NC):
                        sp.wait_ge(S["l0_sum"], e * L0 + i - len(NC) + 1)
                    sp.dma_start(zt[:, k, 0:w], R_dram[bass.ds(e, 1), c, k, :, 0:w].rearrange("o p n -> (o p) n")
                                 ).then_inc(r_in[k], 16)
            for t in range(NT):
                sp.wait_ge(S["tile_done"], CREDIT + (E - 1) * NT + t + 1)
                sp.dma_start(out[t * P:t * P + ROWS[t], :], acc[0:ROWS[t], t, :]).then_inc(S["out_done"], 16)
            sp.wait_ge(S["out_done"], 16 * NT)

        @block.gpsimd
        def _(pool):
            nc.gpsimd.memset(ident[:], 0.0).then_inc(S["ident_ready"], 1)
            pool.wait_ge(S["ident_ready"], 1)
            nc.gpsimd.affine_select(out=ident[:], in_=ident[:], compare_op=ALU.not_equal, fill=1.0, base=0,
                                    pattern=[[-1, P]], channel_multiplier=1).then_inc(S["ident_ready"], 1)
            nc.gpsimd.iota(iota_i, pattern=[[1, AW]], base=0, channel_multiplier=0).then_inc(S["iota_ready"], 1)
            nc.gpsimd.memset(C.ap().bitcast(F32), 0.0).then_inc(S["C_zero"], 1)

            def wait_and_load(q):
                if q == 0:
                    pool.wait_ge(S["edges_T"], 1)
                else:
                    pool.wait_ge(S["Whi_ready"], q)
                    pool.wait_ge(S["Wlo_ready"], q)
                if q == 1:
                    pool.wait_ge(S["wb_lo"], NB)
                pool.dma_start(W32v[:, 0], Wl_q[q]).then_inc(S["w_in"], 16)
                if q % 2 == 1:
                    pool.dma_start(W32v[:, 1], Wr_q[q]).then_inc(S["w_in"], 16)

            def all_max(q):
                pool.wait_ge(S["wmax_ready"], q + 1)
                nc.gpsimd.partition_all_reduce(wmaxA[:], wmax[:], P, bass.bass_isa.ReduceOp.max
                                               ).then_inc(S["wmax_all"], 1)

            wait_and_load(0)
            pool.wait_ge(S["bmax_ready"], 1)
            nc.gpsimd.partition_all_reduce(bmaxA[:], bmax[:], P, bass.bass_isa.ReduceOp.max
                                           ).then_inc(S["bmax_all"], 1)
            all_max(0)
            for b in range(NB):
                pool.wait_ge(S["wbmax_ready"], b + 1)
                nc.gpsimd.partition_all_reduce(wrA[:, b:b + 1], wbmax[:, b % 2:b % 2 + 1], P,
                                               bass.bass_isa.ReduceOp.max).then_inc(S["wbmax_all"], 1)
            for q in range(1, QN):
                wait_and_load(q)
                all_max(q)

        @block.scalar
        def _(act):
            act.wait_ge(S["bn_done"], 1)
            nc.scalar.activation(rs[:, 1, :], rs[:, 0, :], ACT.Sqrt).then_inc(S["sqrt_done"], 1)
            for t in range(NT):
                r = ROWS[t]
                act.wait_ge(S["xn_ready"], t + 1)
                if t >= 2:
                    act.wait_ge(S["h16lo_ready"], t - 1)
                    act.wait_ge(S["hT_ps"], t - 1)
                nc.scalar.activation(h32[0:r, t % 2, :], h32[0:r, t % 2, :], ACT.Relu).then_inc(S["h32_ready"], 1)
                act.wait_ge(S["h32_ready"], t + 1)
                nc.scalar.activation(y[0:r, 0, t, :], h32[0:r, t % 2, :], ACT.Copy, scale=HSCALE
                                     ).then_inc(S["h16hi_ready"], 1)
                act.wait_ge(S["hT_ps"], t + 1)
                pv = ps_z[t % 2][:, :].rearrange("p (c n) -> p c n", c=FC)[:, :, 0:r]
                nc.scalar.activation(hT32[:, :, t * P:t * P + r], pv, ACT.Copy).then_inc(S["hT32_ready"], 1)
                nc.scalar.activation(hT[:, 0, :, t * P:t * P + r], pv, ACT.Copy, scale=HSCALE
                                     ).then_inc(S["hThi_ready"], 1)
            act.wait_ge(S["gates_done"], 1)
            nc.scalar.activation(logit[:], logit[:], ACT.Exp).then_inc(S["exp_done"], 1)

            def split_hi(q, l):
                act.wait_ge(S["scale_ready"], q + 1)
                if l == 0:
                    nc.scalar.activation(W16a[:, 0, :, :].rearrange("p c d -> p (c d)"), W32[:, 0, :],
                                         ACT.Copy, scale=sc[:, 0:1]).then_inc(S["Whi_ready"], 1)
                else:
                    nc.scalar.activation(W16b[:, 0, :, :, :].rearrange("p a c d -> p (a c d)"), w32_flat,
                                         ACT.Copy, scale=sc[:, 3:4]).then_inc(S["Whi_ready"], 1)

            split_hi(0, 0)

            def block_hi(b, s):
                act.wait_ge(S["wb_scale"], b + 1)
                nc.scalar.activation(Wb16[:, s, 0, :, :].rearrange("p c m -> p (c m)"), Wst[:, s, :], ACT.Copy,
                                     scale=bsc[:, s, 0:1]).then_inc(S["wb_hi"], 1)

            def r_out(b, s, k):
                w = NC[k][1]
                act.wait_ge(S["r_full"], b * len(NC) + k + 1)
                act.wait_ge(r_stored[k], 16 * (b + 1))
                nc.scalar.activation(tmp32[:, k, 0:w], ps_r[k][:, 0:w], ACT.Copy, scale=bsc[:, s, 1:2]
                                     ).then_inc(S["r_evac"], 1)

            def source_rows(u, g):
                act.wait_ge(S["counted"], g + 1)
                for c in range(ACT_B):
                    nc.scalar.activation(absB[:, u % 2, c, :], iota16[0:EP, 0:P], ACT.Abs,
                                         bias=nslo_c[:, c, bass.ds(g, 1)]).then_inc(S["absB_ready"], 1)
                act.wait_ge(S["absB_ready"], ACT_B * (g + 1))
                nc.scalar.activation(hotB[:, u, 0:ACT_B, :], absB[:, u % 2, :, :], ACT.Relu, scale=-1.0,
                                     bias=ones32[0:EP, :]).then_inc(S["hotB_ready"], 1)

            def block(b, s, rows, last):
                for u in range(SLOTS):
                    if rows and not (last and u + 2 >= SLOTS):
                        source_rows((u + 2) % SLOTS, b * SLOTS + u + 2)
                    if u >= 1:
                        r_out(b, s, u - 1)
                    if u == 2 and not last:
                        block_hi(b + 1, 1 - s)

            def blocks(rows):
                with act.Fori(0, NB // 2 - 1) as i:
                    block(i * 2, 0, rows, False)
                    block(i * 2 + 1, 1, rows, False)
                block(NB - 2, 0, rows, False)
                block(NB - 1, 1, rows, True)

            block_hi(0, 0)
            act.wait_ge(S["flag_ready"], 1)
            act.wait_ge(S["nslo_ready"], 1)
            need_slow = act.value_load(flag_i[:], min_val=0, max_val=1)
            with act.If(need_slow == 0):
                source_rows(0, 0)
                source_rows(1, 1)
                blocks(True)
            with act.Else():
                blocks(False)

            for i in range(L0):
                c, k, (n0, w) = i // len(NC), i % len(NC), NC[i % len(NC)]
                act.wait_ge(S["agg0_scaled"], i + 1)
                nc.scalar.activation(aT[:, 0, c, n0:n0 + w], tmp32[:, k, 0:w], ACT.Copy
                                     ).then_inc(S["agg0_hi"], 1)

            def expert(e, last):
                for i in range(L0):
                    c, k, (n0, w) = i // len(NC), i % len(NC), NC[i % len(NC)]
                    if i == 0:
                        act.wait_ge(S["t_ready"], CREDIT + e * NT)
                        split_hi(e * 2 + 1, 1)
                    act.wait_ge(S["l0_sum"], e * L0 + i + 1)
                    nc.scalar.activation(h1T[:, 0, c, n0:n0 + w], tmp32[:, k, 0:w], ACT.Relu,
                                         bias=bs[:, c:c + 1], scale=sc[:, 6:7]).then_inc(S["l0_hi"], 1)
                    act.wait_ge(S["l0_hi"], e * L0 + i + 1)
                    nc.scalar.activation(tmp32[:, k, 0:w], tmp32[:, k, 0:w], ACT.Relu,
                                         bias=bs[:, c:c + 1], scale=sc[:, 6:7]).then_inc(S["l0_out"], 1)
                for t in range(NT):
                    i, r = L0 + t, ROWS[t]
                    act.wait_ge(S["ring_full"], L0 + e * RING + i + 1)
                    nc.scalar.activation(y[0:r, 0, t, :], ring[i % SLOTS][0:r, :], ACT.Copy, scale=YSCALE
                                         ).then_inc(S["y_hi"], 1)
                for t in range(NT):
                    r = ROWS[t]
                    act.wait_ge(S["t_ready"], CREDIT + e * NT + t + 1)
                    nc.scalar.activation(zt[0:r, t % 3, :], zt[0:r, t % 3, :], ACT.Relu,
                                         scale=gate_now[0:r, t:t + 1]).then_inc(S["relu_ready"], 1)
                    if t == 0 and not last:
                        split_hi(e * 2 + 2, 0)

            with act.Fori(0, E - 1) as e:
                expert(e, False)
            expert(E - 1, True)

        def slow_columns(dve, V, w):
            def then(ins, k):
                ins.then_inc(S["slow_evac"], 1)
                dve.wait_ge(S["slow_evac"], w * 6 + k)
            inside = zt[0:EP, 0, 0:CH * G].rearrange("p (c g) -> p c g", c=CH)
            below = zt[0:EP, 1, 0:CH * G].rearrange("p (c g) -> p c g", c=CH)
            V.tensor_scalar(below, dst_c, float(WIN), None, ALU.is_lt)
            then(V.tensor_scalar(inside, dst_c, 0.0, None, ALU.is_ge), 1)
            V.tensor_tensor(inside, inside, below, ALU.mult)
            then(V.scalar_tensor_tensor(out=col_c[:], in0=shi_c, scalar=float(WIN), in1=dst_c,
                                        op0=ALU.mult, op1=ALU.add), 2)
            V.scalar_tensor_tensor(out=col_c[:], in0=col_c[:], scalar=1.0, in1=inside,
                                   op0=ALU.add, op1=ALU.mult)
            then(V.tensor_scalar(dst_c, dst_c, -float(WIN), None, ALU.add), 3)
            then(V.tensor_scalar(col_c[:], col_c[:], -1.0, None, ALU.add), 4)

        @block.vector
        def _(dve):
            chain = [0]

            def link(ins):
                chain[0] += 1
                ins.then_inc(S["dve"], 1)
                dve.wait_ge(S["dve"], chain[0])

            V = nc.vector
            for k, n in enumerate(("y_lo", "t_ready", "tile_done", "z_read", "slow_read")):
                V.memset(done_mark[:, k + 2:k + 3], 0.0).then_inc(S[n], CREDIT)
            V.memset(done_mark[:, 7:8], 0.0).then_inc(S["added"], SLOTS)
            V.memset(done_mark[:, 8:9], 0.0).then_inc(S["counted"], SLOTS)
            V.memset(done_mark[:, 9:10], 0.0).then_inc(S["r_evac"], len(NC))
            for k in range(len(NC)):
                V.memset(done_mark[:, 10 + k:11 + k], 0.0).then_inc(r_stored[k], 16)
            V.memset(ones32[:], 1.0)
            V.memset(ones16[:], 1.0)
            V.memset(mv[:], 1.0)
            V.memset(logit[:], 0.0)
            V.memset(inv_col[:], 0.0).then_inc(S["ones_ready"], 1)
            dve.wait_ge(S["iota_ready"], 1)
            V.tensor_copy(iota16[:], iota_i).then_inc(S["iotas_cast"], 1)

            dve.wait_ge(S["dst_in"], 16)
            link(V.tensor_copy(dst_f, dst_i.bitcast(I32)))
            V.tensor_reduce(minmax[:, 0:1], dst_f, AX.X, ALU.min)
            link(V.tensor_reduce(minmax[:, 1:2], dst_f, AX.X, ALU.max))
            dve.wait_ge(S["src_in"], 16)
            link(V.tensor_scalar(shi_i.bitcast(I32), src_i.bitcast(I32), 7, None, ALU.logical_shift_right))
            link(V.tensor_copy(shi_f, shi_i.bitcast(I32)))
            link(V.tensor_scalar(shi_i.bitcast(I32), src_i.bitcast(I32), P - 1, None, ALU.bitwise_and))
            link(V.memset(mm_bc, 0.0))
            V.tensor_scalar(mm_bc[:, 0, :], mm_bc[:, 0, :], minmax[:, 0:1], None, ALU.add)
            V.tensor_scalar(mm_bc[:, 1, :], mm_bc[:, 1, :], minmax[:, 1:2], None, ALU.add)
            V.tensor_copy(slo_f, shi_i.bitcast(I32)).then_inc(S["edges_split"], 1)

            dve.wait_ge(S["edges_T"], 1)
            pc = [ring[k][0:EP, 0:CH * G].rearrange("p (c g) -> p c g", c=CH) for k in range(3)]
            V.tensor_copy(row[0:EP, 0, :], ring[3][0:EP, 0:G])
            V.tensor_copy(row[0:EP, 1, :], ring[3][0:EP, G:2 * G])
            V.tensor_copy(dst_c, pc[0])
            V.tensor_copy(shi_c, pc[1])
            V.tensor_scalar(nslo_c[:], pc[2], -1.0, None, ALU.mult).then_inc(S["nslo_ready"], 1)
            link(V.tensor_copy(slo_c, pc[2]))
            V.tensor_copy(base_i[:], row[0:1, 0, :])
            link(V.scalar_tensor_tensor(out=col_c[:], in0=shi_c, scalar=float(WIN), in1=dst_c,
                                        op0=ALU.mult, op1=ALU.add))
            V.tensor_tensor(col_c[:], col_c[:], row[0:EP, 0:1, :].to_broadcast([EP, CH, G]), ALU.subtract)
            mn, mx = row[0:1, 0, :], row[0:1, 1, :]
            V.tensor_tensor(chk[:, 0, :], mx, mn, ALU.subtract)
            V.tensor_tensor(chk[:, 1, 0:G - 1], mx[:, 0:G - 1], mn[:, 1:G], ALU.subtract)
            link(V.tensor_tensor(chk[:, 2, 0:G - 3], mx[:, 0:G - 3], mn[:, 3:G], ALU.subtract))
            V.tensor_reduce(chk3[:, 0:1], chk[:, 0, :], AX.X, ALU.max)
            V.tensor_reduce(chk3[:, 1:2], chk[:, 1, 0:G - 1], AX.X, ALU.max)
            link(V.tensor_reduce(chk3[:, 2:3], chk[:, 2, 0:G - 3], AX.X, ALU.max))
            V.tensor_scalar(chk3[:, 3:4], chk3[:, 0:1], float(WIN), None, ALU.is_ge)
            V.tensor_scalar(chk3[:, 4:5], chk3[:, 1:2], 0.0, None, ALU.is_gt)
            link(V.tensor_scalar(chk3[:, 5:6], chk3[:, 2:3], 0.0, None, ALU.is_ge))
            link(V.tensor_reduce(chk3[:, 6:7], chk3[:, 3:6], AX.X, ALU.max))
            V.tensor_copy(flag_i[:], chk3[:, 6:7]).then_inc(S["flag_ready"], 1)

            for t in range(NT):
                r = ROWS[t]
                if t % 2 == 0:
                    dve.wait_ge(x_in[t // 2], 16 if ROWS[t + 1] == P else 32)
                ins = V.bn_stats(stats[0:r, t, :], acc[0:r, t, :])
            link(ins)
            for t in range(NT):
                r = ROWS[t]
                ins = V.bn_aggr(mv[0:r, t, :], stats[0:r, t, :])
            link(ins)
            V.tensor_scalar(rs[:, 0, :], mv[:, :, 1], 1e-5, None, ALU.add).then_inc(S["bn_done"], 1)
            dve.wait_ge(S["sqrt_done"], 1)
            link(V.reciprocal(rs[:, 2, :], rs[:, 1, :]))
            link(V.tensor_tensor(rs[:, 3, :], rs[:, 2, :], rs[:, 2, :], ALU.mult))
            link(V.tensor_tensor(rs[:, 3, :], rs[:, 3, :], rs[:, 0, :], ALU.mult))
            link(V.tensor_scalar(rs[:, 3, :], rs[:, 3, :], -0.5, 1.5, ALU.mult, ALU.add))
            link(V.tensor_tensor(rs[:, 2, :], rs[:, 2, :], rs[:, 3, :], ALU.mult))

            def normalize(t):
                r = ROWS[t]
                if t >= 2:
                    dve.wait_ge(S["hT_ps"], t - 1)
                    dve.wait_ge(S["h16lo_ready"], t - 1)
                    dve.wait_ge(S["h16hi_ready"], t - 1)
                V.tensor_scalar(h32[0:r, t % 2, :], acc[0:r, t, :], mv[0:r, t, 0:1], rs[0:r, 2, t:t + 1],
                                ALU.subtract, ALU.mult).then_inc(S["xn_ready"], 1)

            def low_parts(t):
                r = ROWS[t]
                dve.wait_ge(S["h16hi_ready"], t + 1)
                V.scalar_tensor_tensor(out=y[0:r, 1, t, :], in0=h32[0:r, t % 2, :], scalar=HSCALE,
                                       in1=y[0:r, 0, t, :], op0=ALU.mult, op1=ALU.subtract
                                       ).then_inc(S["h16lo_ready"], 1)
                dve.wait_ge(S["hThi_ready"], t + 1)
                V.scalar_tensor_tensor(out=hT[:, 1, :, t * P:t * P + r], in0=hT32[:, :, t * P:t * P + r],
                                       scalar=HSCALE, in1=hT[:, 0, :, t * P:t * P + r],
                                       op0=ALU.mult, op1=ALU.subtract).then_inc(S["hTlo_ready"], 1)

            normalize(0)
            normalize(1)
            for t in range(NT):
                low_parts(t)
                if t + 2 < NT:
                    normalize(t + 2)

            dve.wait_ge(S["b0_ps"], 1)
            link(V.tensor_copy(b0T[:], ps_a[1][:, 0:E * FC]))
            V.tensor_reduce(bmax[:], b0T[:].rearrange("p (e c) -> p e c", c=FC), AX.X, ALU.max,
                            apply_absolute_value=True).then_inc(S["bmax_ready"], 1)

            dve.wait_ge(S["gates_ps"], 1)
            pg = ps_a[0][:, 0:NT * E].rearrange("p (t e) -> p t e", e=E)
            V.tensor_copy(logit[:, 0:NT - 1, :], pg[:, 0:NT - 1, :])
            V.memset(done_mark[:, 15:16], 0.0).then_inc(S["logits_read"], 1)
            link(V.tensor_copy(logit[0:TAIL, NT - 1, :], pg[0:TAIL, NT - 1, :]))
            link(V.tensor_tensor(logit[:], logit[:], gb[:].rearrange("p (o e) -> p o e", o=1
                                                                     ).to_broadcast([P, NT, E]), ALU.add))
            link(V.memset(wins[:], 0.0))
            for i in range(E):
                for j in range(i + 1, E):
                    link(V.tensor_tensor(beat[:, 0, :], logit[:, :, i], logit[:, :, j], ALU.is_ge))
                    V.tensor_tensor(wins[:, :, i], wins[:, :, i], beat[:, 0, :], ALU.add)
                    link(V.tensor_scalar(beat[:, 1, :], beat[:, 0, :], -1.0, 1.0, ALU.mult, ALU.add))
                    link(V.tensor_tensor(wins[:, :, j], wins[:, :, j], beat[:, 1, :], ALU.add))
            link(V.tensor_reduce(gmax[:, :, 0], logit[:], AX.X, ALU.max))
            V.tensor_tensor(logit[:], logit[:], gmax[:].to_broadcast([P, NT, E]), ALU.subtract
                            ).then_inc(S["gates_done"], 1)
            link(V.tensor_scalar(wins[:], wins[:], float(E - 2), None, ALU.is_ge))
            dve.wait_ge(S["exp_done"], 1)
            link(V.tensor_reduce(gsum[:, :, 0], logit[:], AX.X, ALU.add))
            link(V.reciprocal(gsum[:], gsum[:]))
            link(V.tensor_tensor(logit[:], logit[:], gsum[:].to_broadcast([P, NT, E]), ALU.mult))
            link(V.tensor_tensor(gate[:].rearrange("p e t -> p t e"), logit[:], wins[:], ALU.mult))

            def w_max(q, loads, halves):
                dve.wait_ge(S["w_in"], 16 * loads)
                V.tensor_reduce(wmax[:], w32_flat if halves == 2 else W32[:, 0, :], AX.X, ALU.max,
                                apply_absolute_value=True).then_inc(S["wmax_ready"], 1)
                dve.wait_ge(S["wmax_all"], q + 1)

            sci = sc.ap().bitcast(I32)

            def power(then, top, s_at, inv_at, mid):
                then(V.tensor_scalar(sci[:, mid:mid + 1], sci[:, top:top + 1], 0x7F800000, None, ALU.bitwise_and))
                V.tensor_scalar(sci[:, inv_at:inv_at + 1], sci[:, mid:mid + 1], float(-14 * EXP1), None, ALU.add)
                then(V.tensor_scalar(sci[:, s_at:s_at + 1], sci[:, mid:mid + 1], -1.0, float(268 * EXP1),
                                     ALU.mult, ALU.add))

            def scales0(e, then):
                then(V.tensor_scalar(sc[:, 2:3], wmaxA[:], TINY, None, ALU.max))
                power(then, 2, 0, 1, 12)
                then(V.scalar_tensor_tensor(out=sc[:, 9:10], in0=sc[:, 2:3], scalar=float(D),
                                            in1=hbound[:, bass.ds(e, 1)], op0=ALU.mult, op1=ALU.add))
                power(then, 9, 7, 8, 13)

            def scales1(then):
                then(V.tensor_scalar(sc[:, 14:15], wmaxA[:], TINY, None, ALU.max))
                power(then, 14, 3, 4, 15)

            def w_low(layer):
                if layer == 0:
                    return V.scalar_tensor_tensor(
                        out=W16a[:, 1, :, :].rearrange("p c d -> p (c d)"), in0=W32[:, 0, :], scalar=sc[:, 0:1],
                        in1=W16a[:, 0, :, :].rearrange("p c d -> p (c d)"), op0=ALU.mult, op1=ALU.subtract)
                return V.scalar_tensor_tensor(
                    out=W16b[:, 1, :, :, :].rearrange("p a c d -> p (a c d)"), in0=w32_flat, scalar=sc[:, 3:4],
                    in1=W16b[:, 0, :, :, :].rearrange("p a c d -> p (a c d)"), op0=ALU.mult, op1=ALU.subtract)

            w_max(0, 1, 1)
            link(V.tensor_scalar(sc[:, 2:3], wmaxA[:], TINY, None, ALU.max))
            power(link, 2, 0, 1, 12)
            V.memset(done_mark[:, 13:14], 0.0).then_inc(S["scale_ready"], 1)
            dve.wait_ge(S["Whi_ready"], 1)
            w_low(0).then_inc(S["Wlo_ready"], 1)

            def block_max(b, s, loads):
                dve.wait_ge(wst_in[s], 16 * loads)
                V.tensor_reduce(wbmax[:, s:s + 1], Wst[:, s, :], AX.X, ALU.max, apply_absolute_value=True
                                ).then_inc(S["wbmax_ready"], 1)

            bsi = bsc.ap().bitcast(I32)

            def block_scale(b, s):
                def then(ins, k):
                    ins.then_inc(S["wchain"], 1)
                    dve.wait_ge(S["wchain"], b * 2 + k)
                dve.wait_ge(S["wbmax_all"], b + 1)
                then(V.tensor_scalar(bsc[:, s, 2:3], wrA[:, bass.ds(b, 1)], TINY, None, ALU.max), 1)
                then(V.tensor_scalar(bsi[:, s, 3:4], bsi[:, s, 2:3], 0x7F800000, None, ALU.bitwise_and), 2)
                V.tensor_scalar(bsi[:, s, 1:2], bsi[:, s, 3:4], float(-24 * EXP1), None, ALU.add)
                V.tensor_scalar(bsi[:, s, 0:1], bsi[:, s, 3:4], -1.0, float(268 * EXP1), ALU.mult, ALU.add
                                ).then_inc(S["wb_scale"], 1)
                dve.wait_ge(S["wb_scale"], b + 1)

            def block_low(b, s):
                dve.wait_ge(S["wb_hi"], b + 1)
                V.scalar_tensor_tensor(out=Wb16[:, s, 1, :, :].rearrange("p c m -> p (c m)"), in0=Wst[:, s, :],
                                       scalar=bsc[:, s, 0:1], in1=Wb16[:, s, 0, :, :].rearrange("p c m -> p (c m)"),
                                       op0=ALU.mult, op1=ALU.subtract).then_inc(S["wb_lo"], 1)

            block_max(0, 0, 1)
            block_scale(0, 0)
            block_low(0, 0)

            dve.wait_ge(S["C_zero"], 1)
            need_slow = dve.value_load(flag_i[:], min_val=0, max_val=1)

            def one_hots(u, gi, cols, first_b=ACT_B):
                for c in range(CH):
                    ins = V.tensor_scalar(hotA[:, u, c, :], iota16[0:EP, :], cols[:, c, bass.ds(gi, 1)], None,
                                    ALU.is_equal)
                    if c >= first_b:
                        ins = V.tensor_scalar(hotB[:, u, c, :], iota16[0:EP, 0:P],
                                              slo_c[:, c, bass.ds(gi, 1)], None, ALU.is_equal)
                return ins

            def add_counts(u, gi, b):
                dve.wait_ge(S["counted"], SLOTS + gi + 1)
                dve.wait_ge(S["added"], SLOTS + gi)
                dest = C3[:, :, bass.ds(b, WIN)]
                V.tensor_tensor(dest, ring[u][:, 0:AW].rearrange("p (t n) -> p t n", n=WIN), dest, ALU.add
                                ).then_inc(S["added"], 1)

            def load_base(gi):
                return dve.value_load(base_i[0:1, bass.ds(gi, 1)], min_val=0, max_val=N - 1)

            def block(b, s, counts, last):
                for u in range(SLOTS):
                    g = b * SLOTS + u
                    if counts:
                        if not (last and u + 2 >= SLOTS):
                            one_hots((u + 2) % SLOTS, g + 2, col_c).then_inc(S["hot_ready"], 1)
                        add_counts(u, g, load_base(g))
                    if not last:
                        if u == 0:
                            block_max(b + 1, 1 - s, b_loads(b))
                        if u == 1:
                            block_scale(b + 1, 1 - s)
                        if u == 3:
                            block_low(b + 1, 1 - s)

            def blocks(counts):
                with dve.Fori(0, NB // 2 - 1) as i:
                    blocks.loads = i + 1
                    block(i * 2, 0, counts, False)
                    blocks.loads = i + 2
                    block(i * 2 + 1, 1, counts, False)
                blocks.loads = NB // 2
                block(NB - 2, 0, counts, False)
                block(NB - 1, 1, counts, True)

            def b_loads(b):
                return blocks.loads

            with dve.If(need_slow == 0):
                one_hots(0, 0, col_c).then_inc(S["hot_ready"], 1)
                one_hots(1, 1, col_c).then_inc(S["hot_ready"], 1)
                blocks(True)
                dve.wait_ge(S["added"], SLOTS + G)
            with dve.Else():
                with dve.Fori(0, NWIN) as w:
                    slow_columns(dve, V, w)
                    V.memset(done_mark[:, 1:2], 0.0)
                    with dve.Fori(0, G) as g:
                        one_hots(0, g, col_c, 0).then_inc(S["slow_hot"], 1)
                        dve.wait_ge(S["slow_counted"], w * G + g + 1)
                    pw = ring[0][:, 0:AW].rearrange("p (t n) -> p t n", n=WIN)
                    V.tensor_copy(near16, pw).then_inc(S["slow_evac"], 1)
                    dve.wait_ge(S["slow_evac"], w * 6 + 5)
                    V.tensor_copy(C3[:, :, bass.ds(w * WIN, WIN)], near16)
                    V.tensor_tensor(rest8, pw, near16, ALU.subtract, saturate=False).then_inc(S["slow_evac"], 1)
                    dve.wait_ge(S["slow_evac"], w * 6 + 6)
                    V.tensor_copy(R3[:, :, bass.ds(w * WIN, WIN)].bitcast(U8), rest8.bitcast(U8)
                                  ).then_inc(S["slow_read"], 1)
                dve.wait_ge(S["slow_read"], CREDIT + NWIN)
                blocks(False)
            V.memset(done_mark[:, 0:1], 0.0).then_inc(S["C_ready"], 1)

            for k, (n0, w) in enumerate(NC):
                dve.wait_ge(S["deg_ps"], k + 1)
                link(V.tensor_scalar(inv_bc[:, n0:n0 + w], ps_r[k][:, 0:w], 1.0, None, ALU.max))
                link(V.reciprocal(inv_bc[:, n0:n0 + w], inv_bc[:, n0:n0 + w]))
                V.scalar_tensor_tensor(out=inv_bc[:, n0:n0 + w], in0=ps_r[k][:, 0:w], scalar=0.0,
                                       in1=inv_bc[:, n0:n0 + w], op0=ALU.is_gt, op1=ALU.mult
                                       ).then_inc(S["inv_ready"], 1)
            dve.wait_ge(S["inv_ready"], len(NC))
            link(V.tensor_reduce(hbound[:], wrA[:].rearrange("p (e c) -> p e c", c=FC), AX.X, ALU.max))
            dve.wait_ge(S["bmax_all"], 1)
            link(V.scalar_tensor_tensor(out=hbound[:], in0=hbound[:], scalar=float(D), in1=bmaxA[:],
                                        op0=ALU.mult, op1=ALU.add))
            scales0(0, link)
            for k in range(len(NC)):
                dve.wait_ge(r_stored[k], 16 * (NB + 1))

            def agg0_low(i):
                c, k, (n0, w) = i // len(NC), i % len(NC), NC[i % len(NC)]
                dve.wait_ge(S["agg0_hi"], i + 1)
                V.tensor_tensor(aT[:, 1, c, n0:n0 + w], tmp32[:, k, 0:w], aT[:, 0, c, n0:n0 + w],
                                ALU.subtract).then_inc(S["agg0_lo"], 1)

            for i in range(L0):
                c, (n0, w) = i // len(NC), NC[i % len(NC)]
                if i == SLOTS:
                    dve.wait_ge(S["invcol_ps"], 1)
                    V.tensor_copy(inv_col[:, 0:NT - 1], ps_a[1][:, 0:NT - 1])
                    link(V.tensor_copy(inv_col[0:TAIL, NT - 1:NT], ps_a[1][0:TAIL, NT - 1:NT]))
                dve.wait_ge(S["ring_full"], i + 1)
                if i >= 3:
                    dve.wait_ge(S["agg0_lo"], i - 2)
                V.tensor_tensor(tmp32[:, i % 3, 0:w], ring[i % SLOTS][:, 0:w], inv_bc[:, n0:n0 + w], ALU.mult
                                ).then_inc(S["agg0_scaled"], 1)
                if i >= 1:
                    agg0_low(i - 1)
                if i == 6:
                    w_max(1, 3, 2)
                    scales1(link)
                    V.memset(done_mark[:, 14:15], 0.0).then_inc(S["scale_ready"], 1)
            agg0_low(L0 - 1)

            base = chain[0]
            PER = 1 + 1 + 6 + 3

            def expert(e, last):
                cnt = [0]

                def step(ins):
                    cnt[0] += 1
                    ins.then_inc(S["dve"], 1)
                    dve.wait_ge(S["dve"], e * PER + base + cnt[0])

                V.tensor_copy(gate_now[:], gate[:, bass.ds(e, 1), :].rearrange("p o t -> p (o t)"))
                V.tensor_copy(sc[:, 6:7], sc[:, 7:8])
                V.tensor_scalar(sc[:, 10:11], sc[:, 1:2], 1.0 / HSCALE, None, ALU.mult)
                V.tensor_tensor(sc[:, 5:6], sc[:, 4:5], sc[:, 8:9], ALU.mult)
                step(V.tensor_scalar(bs[:], b0T[:, bass.ds(e * FC, FC)], sc[:, 7:8], None, ALU.mult))
                step(V.tensor_scalar(inv_s[:], inv_col[:], sc[:, 5:6], 1.0 / YSCALE, ALU.mult, ALU.mult))

                def l0_low(i):
                    c, k, (n0, w) = i // len(NC), i % len(NC), NC[i % len(NC)]
                    dve.wait_ge(S["l0_out"], e * L0 + i + 1)
                    V.tensor_tensor(h1T[:, 1, c, n0:n0 + w], tmp32[:, k, 0:w], h1T[:, 0, c, n0:n0 + w],
                                    ALU.subtract).then_inc(S["l0_lo"], 1)

                for i in range(L0):
                    c, k, w = i // len(NC), i % len(NC), NC[i % len(NC)][1]
                    dve.wait_ge(S["ring_full"], L0 + e * RING + i + 1)
                    dve.wait_ge(r_in[k], 16 * (e * FC + c + 1))
                    if i >= 3:
                        dve.wait_ge(S["l0_lo"], e * L0 + i - 2)
                    V.scalar_tensor_tensor(out=tmp32[:, k, 0:w], in0=ring[i % SLOTS][:, 0:w], scalar=sc[:, 10:11],
                                           in1=zt[:, k, 0:w], op0=ALU.mult, op1=ALU.add).then_inc(S["l0_sum"], 1)
                    if i >= 1:
                        l0_low(i - 1)
                    if i == 2:
                        dve.wait_ge(S["Whi_ready"], e * 2 + 2)
                        w_low(1).then_inc(S["Wlo_ready"], 1)
                l0_low(L0 - 1)
                for t in range(NT):
                    i, r = L0 + t, ROWS[t]
                    dve.wait_ge(S["y_hi"], e * NT + t + 1)
                    V.scalar_tensor_tensor(out=y[0:r, 1, t, :], in0=ring[i % SLOTS][0:r, :], scalar=YSCALE,
                                           in1=y[0:r, 0, t, :], op0=ALU.mult, op1=ALU.subtract
                                           ).then_inc(S["y_lo"], 1)
                dve.wait_ge(S["b1_in"], 16 * e + 16)

                def add_tile(t):
                    r = ROWS[t]
                    dve.wait_ge(S["relu_ready"], e * NT + t + 1)
                    V.tensor_tensor(acc[0:r, t, :], acc[0:r, t, :], zt[0:r, t % 3, :], ALU.add
                                    ).then_inc(S["tile_done"], 1)

                for t in range(NT):
                    r = ROWS[t]
                    dve.wait_ge(S["z_full"], e * NT + t + 1)
                    dve.wait_ge(S["tile_done"], CREDIT + e * NT + max(t - 2, 0))
                    V.scalar_tensor_tensor(out=zt[0:r, t % 3, :], in0=ps_z[t % 2][0:r, :],
                                           scalar=sc[0:r, 5:6], in1=bias1[0:r, :], op0=ALU.mult, op1=ALU.add
                                           ).then_inc(S["z_read"], 1)
                    dve.wait_ge(S["z_read"], CREDIT + e * NT + t + 1)
                    dve.wait_ge(S["a_full"], e * NT + t + 1)
                    V.scalar_tensor_tensor(out=zt[0:r, t % 3, :], in0=ps_a[t % 2][0:r, :],
                                           scalar=inv_s[0:r, t:t + 1], in1=zt[0:r, t % 3, :],
                                           op0=ALU.mult, op1=ALU.add).then_inc(S["t_ready"], 1)
                    if t >= 1:
                        add_tile(t - 1)
                    if t == 0 and not last:
                        w_max(e * 2 + 2, e * 3 + 4, 1)
                        scales0(e + 1, step)
                        V.memset(done_mark[:, 0:1], 0.0).then_inc(S["scale_ready"], 1)
                    if t == 2 and not last:
                        dve.wait_ge(S["Whi_ready"], e * 2 + 3)
                        w_low(0).then_inc(S["Wlo_ready"], 1)
                    if t == 6 and not last:
                        w_max(e * 2 + 3, e * 3 + 6, 2)
                        scales1(step)
                        V.memset(done_mark[:, 1:2], 0.0).then_inc(S["scale_ready"], 1)
                add_tile(NT - 1)
                assert last or cnt[0] == PER

            with dve.Fori(0, E - 1) as e:
                expert(e, False)
            expert(E - 1, True)

        @block.tensor
        def _(pe):
            T = nc.tensor
            pe.wait_ge(S["ident_ready"], 2)
            pe.wait_ge(S["edges_split"], 1)
            for k, v in enumerate((dst_f, shi_f, slo_f)):
                for c in range(CH):
                    T.transpose(ring[k][0:EP, c * G:(c + 1) * G], v[:, c * EP:(c + 1) * EP], ident[0:G, 0:G])
            T.transpose(ring[3][0:EP, 0:G], mm_bc[:, 0, :], ident[0:G, 0:G])
            T.transpose(ring[3][0:EP, G:2 * G], mm_bc[:, 1, :], ident[0:G, 0:G]).then_inc(S["edges_T"], 1)

            pe.wait_ge(S["consts_in"], 16 * (2 + E))
            T.transpose(ps_a[1][:, 0:E * FC], b_rows[:], ident[0:E * FC, 0:E * FC]).then_inc(S["b0_ps"], 1)

            def gates(t):
                r = ROWS[t]
                pe.wait_ge(S["hT32_ready"], t + 1)
                for c in range(FC):
                    mm = T.matmul(ps_a[0][0:r, t * E:(t + 1) * E], hT32[:, c, t * P:t * P + r], gW[:, c, :],
                                  start=(c == 0), stop=(c == FC - 1))
                return mm

            for t in range(NT):
                r = ROWS[t]
                pe.wait_ge(S["h32_ready"], t + 1)
                if t >= 2:
                    pe.wait_ge(S["hThi_ready"], t - 1)
                for c in range(FC):
                    mm = T.transpose(ps_z[t % 2][:, c * P:c * P + r], h32[0:r, t % 2, c * P:(c + 1) * P],
                                     ident[0:r, 0:r])
                mm.then_inc(S["hT_ps"], 1)
                if t >= 1:
                    gates(t - 1)
            gates(NT - 1).then_inc(S["gates_ps"], 1)

            pe.wait_ge(S["flag_ready"], 1)
            need_slow = pe.value_load(flag_i[:], min_val=0, max_val=1)

            def count(u, start, stop):
                for c in range(CH):
                    mm = T.matmul(ring[u][:, 0:AW], hotB[:, u, c, :], hotA[:, u, c, :],
                                  start=(start and c == 0), stop=(stop and c == CH - 1))
                return mm

            PAIRS = ((0, 0), (0, 1), (1, 0))

            def r_product(b, s, k):
                n0, w = NC[k]
                if k == 0:
                    pe.wait_ge(S["wb_lo"], b + 1)
                pe.wait_ge(S["r_evac"], b * len(NC) + k + 1)
                n = 0
                for f in range(FC):
                    for a, h in PAIRS:
                        mm = T.matmul(ps_r[k][:, 0:w], Wb16[:, s, a, f, :], hT[:, h, f, n0:n0 + w],
                                      start=(n == 0), stop=(n == 3 * FC - 1))
                        n += 1
                mm.then_inc(S["r_full"], 1)

            def pe_block(b, s, counts):
                for u in range(SLOTS):
                    if counts:
                        pe.wait_ge(S["hot_ready"], b * SLOTS + u + 1)
                        pe.wait_ge(S["hotB_ready"], b * SLOTS + u + 1)
                        pe.wait_ge(S["added"], b * SLOTS + u + 1)
                        count(u, True, True).then_inc(S["counted"], 1)
                    if u >= 1:
                        r_product(b, s, u - 1)

            def pe_blocks(counts):
                with pe.Fori(0, NB // 2) as i:
                    pe_block(i * 2, 0, counts)
                    pe_block(i * 2 + 1, 1, counts)

            pe.wait_ge(S["hTlo_ready"], NT)
            pe.wait_ge(S["logits_read"], 1)
            with pe.If(need_slow == 0):
                pe_blocks(True)
            with pe.Else():
                with pe.Fori(0, NWIN) as w:
                    pe.wait_ge(S["slow_read"], CREDIT + w)
                    pe.wait_ge(S["slow_hot"], w * G + 1)
                    count(0, True, False).then_inc(S["slow_counted"], 1)
                    with pe.Fori(1, G - 1) as g:
                        pe.wait_ge(S["slow_hot"], w * G + g + 1)
                        count(0, False, False).then_inc(S["slow_counted"], 1)
                    pe.wait_ge(S["slow_hot"], (w + 1) * G)
                    count(0, False, True).then_inc(S["slow_counted"], 1)
                pe_blocks(False)

            pe.wait_ge(S["C_ready"], 1)
            pe.wait_ge(S["ones_ready"], 1)
            pe.wait_ge(S["r_evac"], len(NC) * (NB + 1))
            for k, (n0, w) in enumerate(NC):
                T.matmul(ps_r[k][:, 0:w], ones16[:], C3[:, 0, n0:n0 + w], start=True, stop=False)
                with pe.If(need_slow != 0):
                    for t in range(NT):
                        T.matmul(ps_r[k][:, 0:w], ones16[0:ROWS[t], :], R3[0:ROWS[t], t, n0:n0 + w],
                                 start=False, stop=False)
                for t in range(1, NT):
                    mm = T.matmul(ps_r[k][:, 0:w], ones16[0:ROWS[t], :], C3[0:ROWS[t], t, n0:n0 + w],
                                  start=False, stop=(t == NT - 1))
                mm.then_inc(S["deg_ps"], 1)

            def inverse_columns():
                pe.wait_ge(S["inv_ready"], len(NC))
                for t in range(NT):
                    mm = T.matmul(ps_a[1][0:ROWS[t], t:t + 1], inv_bc[0:1, t * P:t * P + ROWS[t]],
                                  ident[0:1, 0:1], start=True, stop=True)
                mm.then_inc(S["invcol_ps"], 1)

            pe.wait_ge(S["h16lo_ready"], NT)
            for i in range(L0):
                c, (n0, w) = i // len(NC), NC[i % len(NC)]
                if i == SLOTS:
                    inverse_columns()
                if i >= SLOTS:
                    pe.wait_ge(S["agg0_scaled"], i - SLOTS + 1)

                def part(k, t, M3, start, stop):
                    r = ROWS[t]
                    return T.matmul(ring[i % SLOTS][:, 0:w], y[0:r, k, t, c * P:(c + 1) * P],
                                    M3[0:r, t, n0:n0 + w], start=start, stop=stop)

                part(0, 0, C3, True, False)
                with pe.If(need_slow != 0):
                    for t in range(NT):
                        part(0, t, R3, False, False)
                        part(1, t, R3, False, False)
                part(1, 0, C3, False, False)
                for t in range(1, NT):
                    part(0, t, C3, False, False)
                    mm = part(1, t, C3, False, t == NT - 1)
                mm.then_inc(S["ring_full"], 1)


            def expert(e, last):
                pe.wait_ge(S["Wlo_ready"], e * 2 + 1)
                pe.wait_ge(S["y_lo"], CREDIT + e * NT)
                pe.wait_ge(S["agg0_lo"], L0)
                for i in range(L0):
                    c, (n0, w) = i // len(NC), NC[i % len(NC)]
                    if i >= SLOTS:
                        pe.wait_ge(S["l0_sum"], e * L0 + i - SLOTS + 1)
                    n = 0
                    for k in range(FC):
                        for a, b in PAIRS:
                            mm = T.matmul(ring[i % SLOTS][:, 0:w], W16a[:, a, k, c * P:(c + 1) * P],
                                          aT[:, b, k, n0:n0 + w], start=(n == 0), stop=(n == 3 * FC - 1))
                            n += 1
                    mm.then_inc(S["ring_full"], 1)
                pe.wait_ge(S["Wlo_ready"], e * 2 + 2)
                for t in range(NT):
                    i, r = L0 + t, ROWS[t]
                    ready = L0 - sum(n0 >= t * P + r for n0, _ in NC)
                    pe.wait_ge(S["l0_lo"], e * L0 + ready)
                    if t < SLOTS:
                        pe.wait_ge(S["l0_sum"], e * L0 + i - SLOTS + 1)
                    else:
                        pe.wait_ge(S["y_lo"], CREDIT + e * NT + t - SLOTS + 1)
                    n = 0
                    for k in range(FC):
                        for a, b in PAIRS:
                            mm = T.matmul(ring[i % SLOTS][0:r, :], h1T[:, b, k, t * P:t * P + r],
                                          W16b[:, a, 0, k, :], start=(n == 0), stop=(n == 3 * FC - 1))
                            n += 1
                    mm.then_inc(S["ring_full"], 1)
                for t in range(NT):
                    r = ROWS[t]
                    if t < 2:
                        pe.wait_ge(S["t_ready"], CREDIT + e * NT)
                    else:
                        pe.wait_ge(S["z_read"], CREDIT + e * NT + t - 1)
                    n = 0
                    for k in range(FC):
                        for a, b in PAIRS:
                            mm = T.matmul(ps_z[t % 2][0:r, :], h1T[:, b, k, t * P:t * P + r],
                                          W16b[:, a, 1, k, :], start=(n == 0), stop=(n == 3 * FC - 1))
                            n += 1
                    mm.then_inc(S["z_full"], 1)
                    if t == 0:
                        pe.wait_ge(S["y_lo"], CREDIT + (e + 1) * NT)
                    if t >= 2:
                        pe.wait_ge(S["t_ready"], CREDIT + e * NT + t - 1)

                    def part(k, s, M3, start, stop):
                        q = ROWS[s]
                        return T.matmul(ps_a[t % 2][0:r, :], M3[0:q, s, t * P:t * P + r], y[0:q, k, s, :],
                                        start=start, stop=stop)

                    part(0, 0, C3, True, False)
                    with pe.If(need_slow != 0):
                        for s in range(NT):
                            part(0, s, R3, False, False)
                            part(1, s, R3, False, False)
                    part(1, 0, C3, False, False)
                    for s in range(1, NT):
                        part(0, s, C3, False, False)
                        mm = part(1, s, C3, False, s == NT - 1)
                    mm.then_inc(S["a_full"], 1)

            with pe.Fori(0, E - 1) as e:
                expert(e, False)
            expert(E - 1, True)


_INS = ["x", "src", "dst", "L0_gnn_gate_W", "L0_gnn_gate_b", "L0_gnn_Wl", "L0_gnn_bl", "L0_gnn_Wr"]
_OUTS = [((1250, 512), "float32")]


def kernel(**inputs):
    import numpy as _np
    import concourse.bacc as _bacc
    from concourse import mybir as _mybir
    from concourse.bass_utils import run_bass_kernel_spmd as _run

    nc = _bacc.Bacc("TRN2", target_bir_lowering=False, num_devices=1)
    arrays, args = {}, []
    for name in _INS:
        a = _np.ascontiguousarray(inputs[name])
        arrays[f"in_{name}_dram"] = a
        args.append(nc.dram_tensor(f"in_{name}_dram", a.shape, _mybir.dt.from_np(a.dtype), kind="ExternalInput").ap())
    for i, (shape, dtype) in enumerate(_OUTS):
        dt = _mybir.dt.from_np(_np.dtype(dtype))
        args.append(nc.dram_tensor(f"out_{i}_dram", shape, dt, kind="ExternalOutput").ap())
    sage_moe_kernel(nc, *args)
    r = _run(nc, [arrays], core_ids=[0])
    return r.results[0]["out_0_dram"]
```

```python
from contextlib import ExitStack

import concourse.bass as bass
from concourse import mybir

ALU = mybir.AluOpType
ACT = mybir.ActivationFunctionType
AX = mybir.AxisListType
F32 = mybir.dt.float32
F16 = mybir.dt.float16
F8 = mybir.dt.float8e4
I32 = mybir.dt.int32
U8 = mybir.dt.uint8

P = 128
WIN = 48
CREDIT = 1
ACT_B = 4
SLOTS = 4
HSCALE = 1024.0
YSCALE = 2.0 ** -24
EXP1 = 1 << 23
TINY = 2.0 ** -60


def sage_moe_kernel(nc, x, src, dst, gate_W, gate_b, Wl, bl, Wr, out):
    N, D = x.shape
    E, L = Wl.shape[0], Wl.shape[1]
    NE = src.shape[0]
    FC = D // P
    NT = (N + P - 1) // P
    ROWS = [min(P, N - t * P) for t in range(NT)]
    TAIL = ROWS[-1]
    CH = 5
    EP = 125
    EG = CH * EP
    G = NE // EG
    assert G * EG == NE and G == 64 and G % SLOTS == 0
    AW = NT * WIN
    assert AW <= 512
    NWIN = (N + WIN - 1) // WIN
    CW = 1300
    assert CW >= N - 1 + WIN and CW >= NWIN * WIN
    NC = [(0, 417), (417, 417), (834, 416)]
    NCW = 417
    ACT_TILES = range(NT - 6, NT - 1)
    FIRST_FULL = (NCW + P - 1) // P
    L0 = FC * len(NC)
    RING = L0 + NT
    assert RING - SLOTS >= L0 and L0 % 2 == 0 and NT % 2 == 0

    with ExitStack() as ctx:
        def sb(name, shape, dt):
            return ctx.enter_context(nc.sbuf_tensor(name, shape, dt))

        def psum(name, shape, dt=F32):
            return ctx.enter_context(nc.psum_tensor(name, shape, dt))

        def sem(name):
            return ctx.enter_context(nc.semaphore(name))

        ring = [psum(f"ring{i}", [P, 512]) for i in range(SLOTS)]
        ps_z = [psum(f"ps_z{i}", [P, 512]) for i in range(2)]
        ps_a = [psum(f"ps_a{i}", [P, 512]) for i in range(2)]

        C = sb("C", [P, NT * CW], F16)
        C_rest = sb("C_rest", [P, NT * CW], F8)
        hT = sb("hT", [P, 2, FC, N], F16)
        aT = sb("aT", [P, 2, FC, N], F16)
        h1T = sb("h1T", [P, 2, FC, N], F16)
        W16a = sb("W16a", [P, 2, FC, D], F16)
        W16b = sb("W16b", [P, 2, 2, FC, D], F16)
        Wb16 = sb("Wb16", [P, 2, 2, FC, P], F16)
        wrA = sb("wrA", [P, E * FC], F32)
        ones32 = sb("ones32", [P, 1], F32)
        wbmax = sb("wbmax", [P, 2], F32)
        bsc = sb("bsc", [P, 2, 4], F32)
        hbound = sb("hbound", [P, E], F32)
        nslo_c = sb("nslo_c", [EP, CH, G], F32)
        W32 = sb("W32", [P, 2, FC * D], F32)
        acc = sb("acc", [P, NT, D], F32)
        y = sb("y", [P, 2, NT, D], F16)
        tmp32 = sb("tmp32", [P, len(NC), NCW], F32)
        inv_bc = sb("inv_bc", [P, N], F32)
        bias1 = sb("bias1", [P, D], F32)
        zt = sb("zt", [P, 3, D], F32)
        ident = sb("ident", [P, P], F32)
        ones16 = sb("ones16", [P, P], F16)
        iota_i = zt.ap().rearrange("p a d -> p (a d)")[:, 0:AW].bitcast(I32)
        iota16 = sb("iota16", [P, AW], F16)
        minmax = sb("minmax", [G, 2], F32)
        dst_c, shi_c, slo_c = (inv_bc[0:EP, k * CH * G:(k + 1) * CH * G].rearrange("p (c g) -> p c g", c=CH)
                               for k in range(3))
        col_c = sb("col_c", [EP, CH, G], F32)
        row = sb("row", [P, 2, G], F32)
        base_i = sb("base_i", [1, G], I32)
        chk = sb("chk", [1, 3, G], F32)
        chk3 = sb("chk3", [1, 8], F32)
        flag_i = sb("flag_i", [1, 1], I32)
        stats = sb("stats", [P, NT, 6], F32)
        mv = sb("mv", [P, NT, 2], F32)
        neg_mean = sb("neg_mean", [P, NT], F32)
        sq_dev = sb("sq_dev", [P, NT], F32)
        rs = sb("rs", [P, 4, NT], F32)
        gW = sb("gW", [P, FC, E], F32)
        gb = sb("gb", [P, E], F32)
        logit = sb("logit", [P, NT, E], F32)
        wins = sb("wins", [P, NT, E], F32)
        beat = sb("beat", [P, 2, NT], F32)
        gmax = sb("gmax", [P, NT, 1], F32)
        gsum = sb("gsum", [P, NT, 1], F32)
        gate = sb("gate", [P, E, NT], F32)
        gate_now = sb("gate_now", [P, NT], F32)
        inv_col = sb("inv_col", [P, NT], F32)
        inv_s = sb("inv_s", [P, NT], F32)
        b_rows = sb("b_rows", [E * FC, P], F32)
        b0T = sb("b0T", [P, E * FC], F32)
        bmax = sb("bmax", [P, E], F32)
        bmaxA = sb("bmaxA", [P, E], F32)
        bs = sb("bs", [P, FC], F32)
        wmax = sb("wmax", [P, 1], F32)
        wmaxA = sb("wmaxA", [P, 1], F32)
        sc = sb("sc", [P, 16], F32)
        done_mark = sb("done_mark", [1, 16], F32)

        hotA = aT.ap().rearrange("p a c n -> p (a c n)")[0:EP, 0:SLOTS * CH * AW].rearrange(
            "p (u c a) -> p u c a", u=SLOTS, c=CH)
        hotB = W16b.ap().rearrange("p a b c d -> p (a b c d)")[0:EP, 0:SLOTS * CH * P].rearrange(
            "p (u c b) -> p u c b", u=SLOTS, c=CH)
        Wst = W32.ap()[:, 1, 0:2 * FC * P].rearrange("p (s w) -> p s w", s=2)
        w32_flat = W32.ap().rearrange("p a b -> p (a b)")

        def edge_tmp(k):
            return w32_flat[0:G, k * EG:(k + 1) * EG]

        dst_i, src_i, dst_f, shi_f, slo_f = (edge_tmp(k) for k in range(5))
        shi_i = edge_tmp(5)
        slo_i = zt.ap().rearrange("p a d -> p (a d)")[0:G, 512:512 + EG]
        mm_bc = w32_flat[0:G, 6 * EG:6 * EG + 2 * EP].rearrange("p (k e) -> p k e", k=2)
        hT32 = h1T.ap().rearrange("p a c n -> p (a c n)").bitcast(F32).rearrange("p (c n) -> p c n", c=FC)
        absB = zt.ap()[0:EP, 1, 0:ACT_B * P].bitcast(F16).rearrange("p (s c b) -> p s c b", s=2, c=ACT_B)
        near16 = zt.ap()[:, 1, 0:AW // 2].bitcast(F16).rearrange("p (t n) -> p t n", n=WIN)
        rest8 = zt.ap()[:, 2, 0:AW // 4].bitcast(F8).rearrange("p (t n) -> p t n", n=WIN)
        R_dram = nc.dram_tensor("R_dram", [E, FC, len(NC), P, NCW], F32, kind="Internal").ap()
        LG, IC = 64, 256
        gT = W16a.ap().rearrange("p a c d -> p (a c d)").bitcast(F32)[0:E, 0:N]
        C3 = C.ap().rearrange("p (t n) -> p t n", t=NT)
        R3 = C_rest.ap().rearrange("p (t n) -> p t n", t=NT)

        names = ("dst_in src_in consts_in w_in b1_in out_done edges_split edges_T edges_cast shi_int "
                 "slo_int ident_ready iota_ready C_zero ones_ready flag_ready dve bn_done sqrt_done "
                 "xn_ready h16hi_ready h16lo_ready hT_ps hT32_ready hThi_ready hTlo_ready gates_ps "
                 "gT_ready logits_ps b0_ps exp_done gates_done hot_ready counted added slow_hot "
                 "slow_counted slow_read slow_evac C_ready deg_ps inv_ready invcol_ps ring_full "
                 "agg0_scaled agg0_hi agg0_lo wmax_ready wmax_all scale_ready Whi_ready Wlo_ready l0_sum "
                 "l0_hi l0_out l0_lo wbmax_ready wbmax_all wb_scale wb_hi wb_lo wchain r_full r_evac "
                 "hotB_ready edge_cols mean_ready dev_ready absB_ready y_hi y_lo z_full a_full z_read "
                 "t_ready relu_ready tile_done bmax_ready bmax_all").split()
        S = {n: sem(n) for n in names}
        wst_in = [sem(f"wst_in{k}") for k in range(2)]
        r_stored = [sem(f"r_stored{k}") for k in range(len(NC))]
        r_in = [sem(f"r_in{k}") for k in range(len(NC))]
        NB = E * FC
        x_in = [sem(f"x_in{j}") for j in range(NT // 2)]

        Wl_q = Wl.rearrange("e l (c p) d -> (e l) p c d", p=P)
        Wr_q = Wr.rearrange("e l (c p) d -> (e l) p c d", p=P)
        W32v = W32.ap().rearrange("p a (c d) -> p a c d", c=FC)
        QN = E * L

        ps_r = (ps_a[0], ps_z[0], ps_z[1])

        block = ctx.enter_context(nc.Block())

        @block.sync
        def _(sp):
            sp.dma_start(dst_i.bitcast(I32), dst.rearrange("(g e) -> g e", e=EG)).then_inc(S["dst_in"], 16)
            sp.dma_start(src_i.bitcast(I32), src.rearrange("(g e) -> g e", e=EG)).then_inc(S["src_in"], 16)
            for j in range(NT // 2):
                t = 2 * j
                if ROWS[t + 1] == P:
                    sp.dma_start(acc[:, t:t + 2, :], x[t * P:(t + 2) * P, :].rearrange("(a p) d -> p a d", p=P)
                                 ).then_inc(x_in[j], 16)
                else:
                    sp.dma_start(acc[:, t, :], x[t * P:(t + 1) * P, :]).then_inc(x_in[j], 16)
                    sp.dma_start(acc[0:TAIL, t + 1, :], x[(t + 1) * P:N, :]).then_inc(x_in[j], 16)
            sp.dma_start(gW[:], gate_W.rearrange("(c p) e -> p c e", p=P)).then_inc(S["consts_in"], 16)
            sp.dma_start(gb[:], gate_b.partition_broadcast(P)).then_inc(S["consts_in"], 16)
            for e in range(E):
                sp.dma_start(b_rows[e * FC:(e + 1) * FC, :], bl[e, 0, :].rearrange("(c p) -> c p", p=P)
                             ).then_inc(S["consts_in"], 16)

            def load_block(b):
                e, c = b // FC, b % FC
                if b >= 2:
                    sp.wait_ge(S["wb_lo"], b - 1)
                sp.dma_start(Wst[:, b % 2, :].rearrange("p (c m) -> p c m", c=FC),
                             Wr[e, 0, :, c * P:(c + 1) * P].rearrange("(c p) m -> p c m", p=P)
                             ).then_inc(wst_in[b % 2], 16)

            sp.wait_ge(S["edges_T"], 1)
            load_block(0)
            load_block(1)
            for b in range(NB):
                for k, (n0, w) in enumerate(NC):
                    sp.wait_ge(S["r_evac"], len(NC) + b * len(NC) + k + 1)
                    sp.dma_start(R_dram[b // FC, b % FC, k, :, 0:w], tmp32[:, k, 0:w]).then_inc(r_stored[k], 16)
                if b + 2 < NB:
                    load_block(b + 2)
            for k in range(len(NC)):
                sp.wait_ge(r_stored[k], 16 * (NB + 1))

            with sp.Fori(0, E) as e:
                for i in range(L0):
                    c, k, w = i // len(NC), i % len(NC), NC[i % len(NC)][1]
                    if i == 0:
                        sp.wait_ge(S["tile_done"], CREDIT + e * NT)
                        sp.dma_start(bias1[:], bl[bass.ds(e, 1), 1, :].rearrange("a d -> (a d)"
                                                                                 ).partition_broadcast(P)
                                     ).then_inc(S["b1_in"], 16)
                    if i >= len(NC):
                        sp.wait_ge(S["l0_sum"], e * L0 + i - len(NC) + 1)
                    sp.dma_start(zt[:, k, 0:w], R_dram[bass.ds(e, 1), c, k, :, 0:w].rearrange("o p n -> (o p) n")
                                 ).then_inc(r_in[k], 16)
            for t in range(NT):
                sp.wait_ge(S["tile_done"], CREDIT + (E - 1) * NT + t + 1)
                sp.dma_start(out[t * P:t * P + ROWS[t], :], acc[0:ROWS[t], t, :]).then_inc(S["out_done"], 16)
            sp.wait_ge(S["out_done"], 16 * NT)

        @block.gpsimd
        def _(pool):
            nc.gpsimd.memset(ident[:], 0.0).then_inc(S["ident_ready"], 1)
            pool.wait_ge(S["ident_ready"], 1)
            nc.gpsimd.affine_select(out=ident[:], in_=ident[:], compare_op=ALU.not_equal, fill=1.0, base=0,
                                    pattern=[[-1, P]], channel_multiplier=1).then_inc(S["ident_ready"], 1)
            nc.gpsimd.iota(iota_i, pattern=[[1, AW]], base=0, channel_multiplier=0).then_inc(S["iota_ready"], 1)
            nc.gpsimd.memset(C.ap().bitcast(F32), 0.0).then_inc(S["C_zero"], 1)

            def wait_and_load(q):
                if q == 0:
                    pool.wait_ge(S["edges_T"], 1)
                else:
                    pool.wait_ge(S["Whi_ready"], q)
                    pool.wait_ge(S["Wlo_ready"], q)
                if q == 1:
                    pool.wait_ge(S["wb_lo"], NB)
                if q % L == 0 and q > 0:
                    pool.wait_ge(S["l0_sum"], q // L * L0)
                pool.dma_start(W32v[:, 0], Wl_q[q]).then_inc(S["w_in"], 16)
                if q % 2 == 1:
                    pool.dma_start(W32v[:, 1], Wr_q[q]).then_inc(S["w_in"], 16)

            def all_max(q):
                pool.wait_ge(S["wmax_ready"], q + 1)
                nc.gpsimd.partition_all_reduce(wmaxA[:], wmax[:], P, bass.bass_isa.ReduceOp.max
                                               ).then_inc(S["wmax_all"], 1)

            wait_and_load(0)
            for b in range(NB):
                pool.wait_ge(S["wbmax_ready"], b + 1)
                nc.gpsimd.partition_all_reduce(wrA[:, b:b + 1], wbmax[:, b % 2:b % 2 + 1], P,
                                               bass.bass_isa.ReduceOp.max).then_inc(S["wbmax_all"], 1)
            pool.wait_ge(S["bmax_ready"], 1)
            nc.gpsimd.partition_all_reduce(bmaxA[:], bmax[:], P, bass.bass_isa.ReduceOp.max
                                           ).then_inc(S["bmax_all"], 1)
            all_max(0)
            for q in range(1, QN):
                wait_and_load(q)
                all_max(q)

        @block.scalar
        def _(act):
            def block_hi(b, s):
                act.wait_ge(S["wb_scale"], b + 1)
                nc.scalar.activation(Wb16[:, s, 0, :, :].rearrange("p c m -> p (c m)"), Wst[:, s, :], ACT.Copy,
                                     scale=bsc[:, s, 0:1]).then_inc(S["wb_hi"], 1)

            act.wait_ge(S["ones_ready"], 1)
            nc.scalar.activation(done_mark[:, 15:16], ones32[0:1, :], ACT.Sqrt)
            act.wait_ge(S["dst_in"], 16)
            nc.scalar.activation(dst_f, dst_i.bitcast(I32), ACT.Copy).then_inc(S["edges_cast"], 1)
            act.wait_ge(S["shi_int"], 1)
            nc.scalar.activation(shi_f, shi_i.bitcast(I32), ACT.Copy).then_inc(S["edges_cast"], 1)
            act.wait_ge(S["slo_int"], 1)
            nc.scalar.activation(slo_f, slo_i.bitcast(I32), ACT.Copy).then_inc(S["edges_cast"], 1)
            act.wait_ge(S["edges_T"], 1)
            for k, v in enumerate((dst_c, shi_c, nslo_c[:])):
                nc.scalar.activation(v, ring[k][0:EP, 0:CH * G].rearrange("p (c g) -> p c g", c=CH), ACT.Copy,
                                     scale=-1.0 if k == 2 else 1.0).then_inc(S["edge_cols"], 1)
            unread = h1T.ap().rearrange("p a c n -> p (a c n)").bitcast(F32)[:, 0:len(ACT_TILES) * D].rearrange(
                "p (k d) -> p k d", d=D)
            for k, t in enumerate(ACT_TILES):
                r = ROWS[t]
                act.wait_ge(x_in[t // 2], 16 if ROWS[t // 2 * 2 + 1] == P else 32)
                nc.scalar.activation(unread[0:r, k, :], acc[0:r, t, :], ACT.Copy, scale=-1.0 / D,
                                     accum_out=neg_mean[0:r, t:t + 1]).then_inc(S["mean_ready"], 1)
            for k, t in enumerate(ACT_TILES):
                r = ROWS[t]
                act.wait_ge(S["mean_ready"], k + 1)
                nc.scalar.activation(unread[0:r, k, :], acc[0:r, t, :], ACT.Square, bias=neg_mean[0:r, t:t + 1],
                                     accum_out=sq_dev[0:r, t:t + 1]).then_inc(S["dev_ready"], 1)
            block_hi(0, 0)
            act.wait_ge(S["bn_done"], 1)
            nc.scalar.activation(rs[:, 1, :], rs[:, 0, :], ACT.Sqrt).then_inc(S["sqrt_done"], 1)
            def high_parts(t):
                r = ROWS[t]
                act.wait_ge(S["xn_ready"], t + 1)
                nc.scalar.activation(y[0:r, 0, t, :], zt[0:r, t % 3, :], ACT.Relu).then_inc(S["h16hi_ready"], 1)

            def high_parts_T(t):
                r = ROWS[t]
                act.wait_ge(S["hT_ps"], t + 1)
                pv = ps_z[t % 2][:, :].rearrange("p (c n) -> p c n", c=FC)[:, :, 0:r]
                nc.scalar.activation(hT32[:, :, t * P:t * P + r], pv, ACT.Relu).then_inc(S["hT32_ready"], 1)
                nc.scalar.activation(hT[:, 0, :, t * P:t * P + r], pv, ACT.Relu).then_inc(S["hThi_ready"], 1)

            def gates_out(k):
                n0, w = NC[k]
                act.wait_ge(S["gates_ps"], k + 1)
                nc.scalar.activation(gT[:, n0:n0 + w], ring[k][0:E, 0:w], ACT.Copy).then_inc(S["gT_ready"], 1)

            high_parts(0)
            for t in range(NT):
                if t + 1 < NT:
                    high_parts(t + 1)
                high_parts_T(t)
            for k in range(len(NC) - 1):
                gates_out(k)

            def split_hi(q, l):
                act.wait_ge(S["scale_ready"], q + 1)
                if l == 0:
                    nc.scalar.activation(W16a[:, 0, :, :].rearrange("p c d -> p (c d)"), W32[:, 0, :],
                                         ACT.Copy, scale=sc[:, 0:1]).then_inc(S["Whi_ready"], 1)
                else:
                    nc.scalar.activation(W16b[:, 0, :, :, :].rearrange("p a c d -> p (a c d)"), w32_flat,
                                         ACT.Copy, scale=sc[:, 3:4]).then_inc(S["Whi_ready"], 1)

            def r_out(b, s, k):
                w = NC[k][1]
                act.wait_ge(S["r_full"], b * len(NC) + k + 1)
                act.wait_ge(r_stored[k], 16 * (b + 1))
                nc.scalar.activation(tmp32[:, k, 0:w], ps_r[k][:, 0:w], ACT.Copy, scale=bsc[:, s, 1:2]
                                     ).then_inc(S["r_evac"], 1)

            def source_rows(u, g):
                act.wait_ge(S["counted"], g + 1)
                for c in range(ACT_B):
                    nc.scalar.activation(absB[:, u % 2, c, :], iota16[0:EP, 0:P], ACT.Abs,
                                         bias=nslo_c[:, c, bass.ds(g, 1)]).then_inc(S["absB_ready"], 1)
                act.wait_ge(S["absB_ready"], ACT_B * (g + 1))
                nc.scalar.activation(hotB[:, u, 0:ACT_B, :], absB[:, u % 2, :, :], ACT.Relu, scale=-1.0,
                                     bias=ones32[0:EP, :]).then_inc(S["hotB_ready"], 1)

            def block(b, s, rows, last):
                for u in range(SLOTS):
                    if rows and not (last and u + 2 >= SLOTS):
                        source_rows((u + 2) % SLOTS, b * SLOTS + u + 2)
                    if u == 1 and not last:
                        block_hi(b + 1, 1 - s)
                    if u < len(NC):
                        r_out(b, s, u)

            def blocks(rows):
                with act.Fori(0, NB // 2 - 1) as i:
                    block(i * 2, 0, rows, False)
                    block(i * 2 + 1, 1, rows, False)
                block(NB - 2, 0, rows, False)
                block(NB - 1, 1, rows, True)

            act.wait_ge(S["flag_ready"], 1)
            act.wait_ge(S["edge_cols"], 3)
            act.wait_ge(S["h16lo_ready"], NT - 2)
            need_slow = act.value_load(flag_i[:], min_val=0, max_val=1)
            with act.If(need_slow == 0):
                source_rows(0, 0)
                source_rows(1, 1)
                blocks(True)
            with act.Else():
                blocks(False)
            gates_out(len(NC) - 1)

            for i in range(L0):
                c, k, (n0, w) = i // len(NC), i % len(NC), NC[i % len(NC)]
                if i == 3:
                    act.wait_ge(S["logits_ps"], 1)
                    split_hi(0, 0)
                if i == 6:
                    act.wait_ge(S["gates_done"], 1)
                    nc.scalar.activation(logit[:], logit[:], ACT.Exp).then_inc(S["exp_done"], 1)
                act.wait_ge(S["agg0_scaled"], i + 1)
                nc.scalar.activation(aT[:, 0, c, n0:n0 + w], tmp32[:, k, 0:w], ACT.Copy
                                     ).then_inc(S["agg0_hi"], 1)

            def expert(e, last):
                for i in range(L0):
                    c, k, (n0, w) = i // len(NC), i % len(NC), NC[i % len(NC)]
                    if i == 0:
                        act.wait_ge(S["t_ready"], CREDIT + e * NT)
                        split_hi(e * 2 + 1, 1)
                    act.wait_ge(S["l0_sum"], e * L0 + i + 1)
                    nc.scalar.activation(h1T[:, 0, c, n0:n0 + w], tmp32[:, k, 0:w], ACT.Relu,
                                         bias=bs[:, c:c + 1], scale=sc[:, 6:7]).then_inc(S["l0_hi"], 1)
                    act.wait_ge(S["l0_hi"], e * L0 + i + 1)
                    nc.scalar.activation(tmp32[:, k, 0:w], tmp32[:, k, 0:w], ACT.Relu,
                                         bias=bs[:, c:c + 1], scale=sc[:, 6:7]).then_inc(S["l0_out"], 1)
                for t in range(NT):
                    i, r = L0 + t, ROWS[t]
                    act.wait_ge(S["ring_full"], L0 + e * RING + i + 1)
                    nc.scalar.activation(y[0:r, 0, t, :], ring[i % SLOTS][0:r, :], ACT.Copy, scale=YSCALE
                                         ).then_inc(S["y_hi"], 1)
                for t in range(NT):
                    r = ROWS[t]
                    act.wait_ge(S["t_ready"], CREDIT + e * NT + t + 1)
                    nc.scalar.activation(zt[0:r, t % 3, :], zt[0:r, t % 3, :], ACT.Relu,
                                         scale=gate_now[0:r, t:t + 1]).then_inc(S["relu_ready"], 1)
                    if t == 0 and not last:
                        split_hi(e * 2 + 2, 0)

            with act.Fori(0, E - 1) as e:
                expert(e, False)
            expert(E - 1, True)

        def slow_columns(dve, V, w):
            def then(ins, k):
                ins.then_inc(S["slow_evac"], 1)
                dve.wait_ge(S["slow_evac"], w * 6 + k)
            inside = zt[0:EP, 0, 0:CH * G].rearrange("p (c g) -> p c g", c=CH)
            below = zt[0:EP, 1, 0:CH * G].rearrange("p (c g) -> p c g", c=CH)
            V.tensor_scalar(below, dst_c, float(WIN), None, ALU.is_lt)
            then(V.tensor_scalar(inside, dst_c, 0.0, None, ALU.is_ge), 1)
            V.tensor_tensor(inside, inside, below, ALU.mult)
            then(V.scalar_tensor_tensor(out=col_c[:], in0=shi_c, scalar=float(WIN), in1=dst_c,
                                        op0=ALU.mult, op1=ALU.add), 2)
            V.scalar_tensor_tensor(out=col_c[:], in0=col_c[:], scalar=1.0, in1=inside,
                                   op0=ALU.add, op1=ALU.mult)
            then(V.tensor_scalar(dst_c, dst_c, -float(WIN), None, ALU.add), 3)
            then(V.tensor_scalar(col_c[:], col_c[:], -1.0, None, ALU.add), 4)

        @block.vector
        def _(dve):
            chain = [0]

            def link(ins):
                chain[0] += 1
                ins.then_inc(S["dve"], 1)
                dve.wait_ge(S["dve"], chain[0])

            V = nc.vector
            for k, n in enumerate(("y_lo", "t_ready", "tile_done", "z_read", "slow_read")):
                V.memset(done_mark[:, k + 2:k + 3], 0.0).then_inc(S[n], CREDIT)
            V.memset(done_mark[:, 7:8], 0.0).then_inc(S["added"], SLOTS)
            V.memset(done_mark[:, 8:9], 0.0).then_inc(S["counted"], SLOTS)
            V.memset(done_mark[:, 9:10], 0.0).then_inc(S["r_evac"], len(NC))
            for k in range(len(NC)):
                V.memset(done_mark[:, 10 + k:11 + k], 0.0).then_inc(r_stored[k], 16)
            V.memset(ones32[:], 1.0)
            V.memset(ones16[:], 1.0)
            V.memset(mv[:], 1.0)
            V.memset(logit[:], 0.0)
            V.memset(inv_col[:], 0.0).then_inc(S["ones_ready"], 1)
            dve.wait_ge(S["iota_ready"], 1)
            V.tensor_copy(iota16[:], iota_i)

            dve.wait_ge(S["src_in"], 16)
            V.tensor_scalar(shi_i.bitcast(I32), src_i.bitcast(I32), 7, None, ALU.logical_shift_right
                            ).then_inc(S["shi_int"], 1)
            V.tensor_scalar(slo_i.bitcast(I32), src_i.bitcast(I32), P - 1, None, ALU.bitwise_and
                            ).then_inc(S["slo_int"], 1)
            link(V.memset(mm_bc, 0.0))
            dve.wait_ge(S["edges_cast"], 1)
            V.tensor_reduce(minmax[:, 0:1], dst_f, AX.X, ALU.min)
            link(V.tensor_reduce(minmax[:, 1:2], dst_f, AX.X, ALU.max))
            V.tensor_scalar(mm_bc[:, 0, :], mm_bc[:, 0, :], minmax[:, 0:1], None, ALU.add)
            V.tensor_scalar(mm_bc[:, 1, :], mm_bc[:, 1, :], minmax[:, 1:2], None, ALU.add
                            ).then_inc(S["edges_split"], 1)

            dve.wait_ge(S["edges_T"], 1)
            V.tensor_copy(row[0:EP, 0, :], ring[3][0:EP, 0:G])
            link(V.tensor_copy(row[0:EP, 1, :], ring[3][0:EP, G:2 * G]))
            V.tensor_copy(base_i[:], row[0:1, 0, :])
            dve.wait_ge(S["edge_cols"], 2)
            link(V.scalar_tensor_tensor(out=col_c[:], in0=shi_c, scalar=float(WIN), in1=dst_c,
                                        op0=ALU.mult, op1=ALU.add))
            V.tensor_tensor(col_c[:], col_c[:], row[0:EP, 0:1, :].to_broadcast([EP, CH, G]), ALU.subtract)
            mn, mx = row[0:1, 0, :], row[0:1, 1, :]
            V.tensor_tensor(chk[:, 0, :], mx, mn, ALU.subtract)
            V.tensor_tensor(chk[:, 1, 0:G - 1], mx[:, 0:G - 1], mn[:, 1:G], ALU.subtract)
            link(V.tensor_tensor(chk[:, 2, 0:G - 3], mx[:, 0:G - 3], mn[:, 3:G], ALU.subtract))
            V.tensor_reduce(chk3[:, 0:1], chk[:, 0, :], AX.X, ALU.max)
            V.tensor_reduce(chk3[:, 1:2], chk[:, 1, 0:G - 1], AX.X, ALU.max)
            link(V.tensor_reduce(chk3[:, 2:3], chk[:, 2, 0:G - 3], AX.X, ALU.max))
            V.tensor_scalar(chk3[:, 3:4], chk3[:, 0:1], float(WIN), None, ALU.is_ge)
            V.tensor_scalar(chk3[:, 4:5], chk3[:, 1:2], 0.0, None, ALU.is_gt)
            link(V.tensor_scalar(chk3[:, 5:6], chk3[:, 2:3], 0.0, None, ALU.is_ge))
            link(V.tensor_reduce(chk3[:, 6:7], chk3[:, 3:6], AX.X, ALU.max))
            V.tensor_copy(flag_i[:], chk3[:, 6:7]).then_inc(S["flag_ready"], 1)

            dve.wait_ge(S["edge_cols"], 3)
            V.tensor_scalar(slo_c, nslo_c[:], -1.0, None, ALU.mult)

            def block_max(b, s, loads):
                dve.wait_ge(wst_in[s], 16 * loads)
                V.tensor_reduce(wbmax[:, s:s + 1], Wst[:, s, :], AX.X, ALU.max, apply_absolute_value=True
                                ).then_inc(S["wbmax_ready"], 1)

            bsi = bsc.ap().bitcast(I32)

            def block_scale(b, s):
                def then(ins, k):
                    ins.then_inc(S["wchain"], 1)
                    dve.wait_ge(S["wchain"], b * 2 + k)
                dve.wait_ge(S["wbmax_all"], b + 1)
                then(V.tensor_scalar(bsc[:, s, 2:3], wrA[:, bass.ds(b, 1)], TINY, None, ALU.max), 1)
                then(V.tensor_scalar(bsi[:, s, 3:4], bsi[:, s, 2:3], 0x7F800000, None, ALU.bitwise_and), 2)
                V.tensor_scalar(bsi[:, s, 1:2], bsi[:, s, 3:4], float(-24 * EXP1), None, ALU.add)
                V.tensor_scalar(bsi[:, s, 0:1], bsi[:, s, 3:4], -1.0, float(268 * EXP1), ALU.mult, ALU.add
                                ).then_inc(S["wb_scale"], 1)
                dve.wait_ge(S["wb_scale"], b + 1)

            def block_low(b, s):
                dve.wait_ge(S["wb_hi"], b + 1)
                V.scalar_tensor_tensor(out=Wb16[:, s, 1, :, :].rearrange("p c m -> p (c m)"), in0=Wst[:, s, :],
                                       scalar=bsc[:, s, 0:1], in1=Wb16[:, s, 0, :, :].rearrange("p c m -> p (c m)"),
                                       op0=ALU.mult, op1=ALU.subtract).then_inc(S["wb_lo"], 1)

            block_max(0, 0, 1)
            own_tiles = [t for t in range(NT) if t not in ACT_TILES]
            for t in own_tiles:
                r = ROWS[t]
                dve.wait_ge(x_in[t // 2], 16 if ROWS[t // 2 * 2 + 1] == P else 32)
                ins = V.bn_stats(stats[0:r, t, :], acc[0:r, t, :])
            link(ins)
            block_scale(0, 0)
            for t in own_tiles:
                r = ROWS[t]
                V.bn_aggr(mv[0:r, t, :], stats[0:r, t, :])
            dve.wait_ge(S["dev_ready"], len(ACT_TILES))
            a0, a1 = ACT_TILES[0], ACT_TILES[-1] + 1
            V.tensor_scalar(mv[:, a0:a1, 0], neg_mean[:, a0:a1], -1.0, None, ALU.mult)
            link(V.tensor_scalar(mv[:, a0:a1, 1], sq_dev[:, a0:a1], 1.0 / D, None, ALU.mult))
            V.tensor_scalar(rs[:, 0, :], mv[:, :, 1], 1e-5, None, ALU.add).then_inc(S["bn_done"], 1)
            dve.wait_ge(S["sqrt_done"], 1)
            link(V.reciprocal(rs[:, 2, :], rs[:, 1, :]))
            link(V.tensor_tensor(rs[:, 3, :], rs[:, 2, :], rs[:, 2, :], ALU.mult))
            link(V.tensor_tensor(rs[:, 3, :], rs[:, 3, :], rs[:, 0, :], ALU.mult))
            link(V.tensor_scalar(rs[:, 3, :], rs[:, 3, :], -0.5, 1.5, ALU.mult, ALU.add))
            link(V.scalar_tensor_tensor(out=rs[:, 2, :], in0=rs[:, 2, :], scalar=HSCALE, in1=rs[:, 3, :],
                                        op0=ALU.mult, op1=ALU.mult))

            def normalize(t):
                r = ROWS[t]
                if t >= 3:
                    dve.wait_ge(S["hT_ps"], t - 2)
                    dve.wait_ge(S["h16lo_ready"], t - 2)
                V.tensor_scalar(zt[0:r, t % 3, :], acc[0:r, t, :], mv[0:r, t, 0:1], rs[0:r, 2, t:t + 1],
                                ALU.subtract, ALU.mult).then_inc(S["xn_ready"], 1)

            def low_parts(t):
                r = ROWS[t]
                dve.wait_ge(S["h16hi_ready"], t + 1)
                V.scalar_tensor_tensor(out=y[0:r, 1, t, :], in0=zt[0:r, t % 3, :], scalar=0.0,
                                       in1=y[0:r, 0, t, :], op0=ALU.max, op1=ALU.subtract
                                       ).then_inc(S["h16lo_ready"], 1)

            def low_parts_T(t):
                r = ROWS[t]
                dve.wait_ge(S["hThi_ready"], t + 1)
                V.tensor_tensor(hT[:, 1, :, t * P:t * P + r], hT32[:, :, t * P:t * P + r],
                                hT[:, 0, :, t * P:t * P + r], ALU.subtract).then_inc(S["hTlo_ready"], 1)

            dve.wait_ge(S["edges_cast"], 3)
            for t in range(3):
                normalize(t)
            block_low(0, 0)
            for t in range(NT):
                low_parts(t)
                if t >= 1:
                    low_parts_T(t - 1)
                if t + 3 < NT:
                    normalize(t + 3)
            low_parts_T(NT - 1)

            def w_max(q, loads, halves):
                dve.wait_ge(S["w_in"], 16 * loads)
                V.tensor_reduce(wmax[:], w32_flat if halves == 2 else W32[:, 0, :], AX.X, ALU.max,
                                apply_absolute_value=True).then_inc(S["wmax_ready"], 1)
                dve.wait_ge(S["wmax_all"], q + 1)

            sci = sc.ap().bitcast(I32)

            def power(then, top, s_at, inv_at, mid):
                then(V.tensor_scalar(sci[:, mid:mid + 1], sci[:, top:top + 1], 0x7F800000, None, ALU.bitwise_and))
                V.tensor_scalar(sci[:, inv_at:inv_at + 1], sci[:, mid:mid + 1], float(-14 * EXP1), None, ALU.add)
                then(V.tensor_scalar(sci[:, s_at:s_at + 1], sci[:, mid:mid + 1], -1.0, float(268 * EXP1),
                                     ALU.mult, ALU.add))

            def scales0(e, then):
                then(V.tensor_scalar(sc[:, 2:3], wmaxA[:], TINY, None, ALU.max))
                power(then, 2, 0, 1, 12)
                then(V.scalar_tensor_tensor(out=sc[:, 9:10], in0=sc[:, 2:3], scalar=float(D),
                                            in1=hbound[:, bass.ds(e, 1)], op0=ALU.mult, op1=ALU.add))
                power(then, 9, 7, 8, 13)

            def scales1(then):
                then(V.tensor_scalar(sc[:, 14:15], wmaxA[:], TINY, None, ALU.max))
                power(then, 14, 3, 4, 15)

            def w_low(layer):
                if layer == 0:
                    return V.scalar_tensor_tensor(
                        out=W16a[:, 1, :, :].rearrange("p c d -> p (c d)"), in0=W32[:, 0, :], scalar=sc[:, 0:1],
                        in1=W16a[:, 0, :, :].rearrange("p c d -> p (c d)"), op0=ALU.mult, op1=ALU.subtract)
                m = layer - 1
                return V.scalar_tensor_tensor(
                    out=W16b[:, 1, m, :, :].rearrange("p c d -> p (c d)"), in0=W32[:, m, :], scalar=sc[:, 3:4],
                    in1=W16b[:, 0, m, :, :].rearrange("p c d -> p (c d)"), op0=ALU.mult, op1=ALU.subtract)

            dve.wait_ge(S["C_zero"], 1)
            need_slow = dve.value_load(flag_i[:], min_val=0, max_val=1)

            def one_hots(u, gi, cols, first_b=ACT_B):
                for c in range(CH):
                    ins = V.tensor_scalar(hotA[:, u, c, :], iota16[0:EP, :], cols[:, c, bass.ds(gi, 1)], None,
                                    ALU.is_equal)
                    if c >= first_b:
                        ins = V.tensor_scalar(hotB[:, u, c, :], iota16[0:EP, 0:P],
                                              slo_c[:, c, bass.ds(gi, 1)], None, ALU.is_equal)
                return ins

            def add_counts(u, gi, b):
                dve.wait_ge(S["counted"], SLOTS + gi + 1)
                dve.wait_ge(S["added"], SLOTS + gi)
                dest = C3[:, :, bass.ds(b, WIN)]
                V.tensor_tensor(dest, ring[u][:, 0:AW].rearrange("p (t n) -> p t n", n=WIN), dest, ALU.add
                                ).then_inc(S["added"], 1)

            def load_base(gi):
                return dve.value_load(base_i[0:1, bass.ds(gi, 1)], min_val=0, max_val=N - 1)

            def block(b, s, loads, counts, last):
                for u in range(SLOTS):
                    g = b * SLOTS + u
                    if u == 0 and not last:
                        block_max(b + 1, 1 - s, loads)
                    if u == 1 and not last:
                        block_scale(b + 1, 1 - s)
                    if u == 2 and not last:
                        block_low(b + 1, 1 - s)
                    if counts:
                        if not (last and u + 2 >= SLOTS):
                            one_hots((u + 2) % SLOTS, g + 2, col_c).then_inc(S["hot_ready"], 1)
                    if counts:
                        add_counts(u, g, load_base(g))

            def blocks(counts):
                with dve.Fori(0, NB // 2 - 1) as i:
                    block(i * 2, 0, i + 1, counts, False)
                    block(i * 2 + 1, 1, i + 2, counts, False)
                block(NB - 2, 0, NB // 2, counts, False)
                block(NB - 1, 1, 0, counts, True)

            with dve.If(need_slow == 0):
                one_hots(0, 0, col_c).then_inc(S["hot_ready"], 1)
                one_hots(1, 1, col_c).then_inc(S["hot_ready"], 1)
                blocks(True)
                dve.wait_ge(S["added"], SLOTS + G)
            with dve.Else():
                dve.wait_ge(S["h16lo_ready"], NT)
                dve.wait_ge(S["hT_ps"], NT)
                with dve.Fori(0, NWIN) as w:
                    slow_columns(dve, V, w)
                    V.memset(done_mark[:, 1:2], 0.0)
                    with dve.Fori(0, G) as g:
                        one_hots(0, g, col_c, 0).then_inc(S["slow_hot"], 1)
                        dve.wait_ge(S["slow_counted"], w * G + g + 1)
                    pw = ring[0][:, 0:AW].rearrange("p (t n) -> p t n", n=WIN)
                    V.tensor_copy(near16, pw).then_inc(S["slow_evac"], 1)
                    dve.wait_ge(S["slow_evac"], w * 6 + 5)
                    V.tensor_copy(C3[:, :, bass.ds(w * WIN, WIN)], near16)
                    V.tensor_tensor(rest8, pw, near16, ALU.subtract, saturate=False).then_inc(S["slow_evac"], 1)
                    dve.wait_ge(S["slow_evac"], w * 6 + 6)
                    V.tensor_copy(R3[:, :, bass.ds(w * WIN, WIN)].bitcast(U8), rest8.bitcast(U8)
                                  ).then_inc(S["slow_read"], 1)
                dve.wait_ge(S["slow_read"], CREDIT + NWIN)
                blocks(False)
            V.memset(done_mark[:, 0:1], 0.0).then_inc(S["C_ready"], 1)

            dve.wait_ge(S["b0_ps"], 1)
            link(V.tensor_copy(b0T[:], ps_a[1][:, 0:E * FC]))
            V.tensor_reduce(bmax[:], b0T[:].rearrange("p (e c) -> p e c", c=FC), AX.X, ALU.max,
                            apply_absolute_value=True).then_inc(S["bmax_ready"], 1)

            for k, (n0, w) in enumerate(NC):
                dve.wait_ge(S["deg_ps"], k + 1)
                link(V.tensor_scalar(inv_bc[:, n0:n0 + w], ps_r[k][:, 0:w], 1.0, None, ALU.max))
                link(V.reciprocal(inv_bc[:, n0:n0 + w], inv_bc[:, n0:n0 + w]))
                V.scalar_tensor_tensor(out=inv_bc[:, n0:n0 + w], in0=ps_r[k][:, 0:w], scalar=0.0,
                                       in1=inv_bc[:, n0:n0 + w], op0=ALU.is_gt, op1=ALU.mult
                                       ).then_inc(S["inv_ready"], 1)
            dve.wait_ge(S["inv_ready"], len(NC))
            w_max(0, 1, 1)
            link(V.tensor_reduce(hbound[:], wrA[:].rearrange("p (e c) -> p e c", c=FC), AX.X, ALU.max))
            dve.wait_ge(S["bmax_all"], 1)
            link(V.scalar_tensor_tensor(out=hbound[:], in0=hbound[:], scalar=float(D), in1=bmaxA[:],
                                        op0=ALU.mult, op1=ALU.add))
            scales0(0, link)
            V.memset(done_mark[:, 13:14], 0.0).then_inc(S["scale_ready"], 1)
            for k in range(len(NC)):
                dve.wait_ge(r_stored[k], 16 * (NB + 1))

            def gates_before_exp():
                dve.wait_ge(S["logits_ps"], 1)
                pg = ps_a[1][:, LG:LG + NT * E].rearrange("p (t e) -> p t e", e=E)
                V.tensor_scalar(logit[:, 0:NT - 1, :], pg[:, 0:NT - 1, :], 1.0 / HSCALE, None, ALU.mult)
                link(V.tensor_scalar(logit[0:TAIL, NT - 1, :], pg[0:TAIL, NT - 1, :], 1.0 / HSCALE, None, ALU.mult))
                link(V.tensor_tensor(logit[:], logit[:], gb[:].rearrange("p (o e) -> p o e", o=1
                                                                         ).to_broadcast([P, NT, E]), ALU.add))
                link(V.memset(wins[:], 0.0))
                for i in range(E):
                    for j in range(i + 1, E):
                        link(V.tensor_tensor(beat[:, 0, :], logit[:, :, i], logit[:, :, j], ALU.is_ge))
                        V.tensor_tensor(wins[:, :, i], wins[:, :, i], beat[:, 0, :], ALU.add)
                        link(V.tensor_scalar(beat[:, 1, :], beat[:, 0, :], -1.0, 1.0, ALU.mult, ALU.add))
                        link(V.tensor_tensor(wins[:, :, j], wins[:, :, j], beat[:, 1, :], ALU.add))
                link(V.tensor_reduce(gmax[:, :, 0], logit[:], AX.X, ALU.max))
                V.tensor_tensor(logit[:], logit[:], gmax[:].to_broadcast([P, NT, E]), ALU.subtract
                                ).then_inc(S["gates_done"], 1)
                link(V.tensor_scalar(wins[:], wins[:], float(E - 2), None, ALU.is_ge))

            def gates_after_exp():
                dve.wait_ge(S["exp_done"], 1)
                link(V.tensor_reduce(gsum[:, :, 0], logit[:], AX.X, ALU.add))
                link(V.reciprocal(gsum[:], gsum[:]))
                link(V.tensor_tensor(logit[:], logit[:], gsum[:].to_broadcast([P, NT, E]), ALU.mult))
                link(V.tensor_tensor(gate[:].rearrange("p e t -> p t e"), logit[:], wins[:], ALU.mult))

            def agg0_low(i):
                c, k, (n0, w) = i // len(NC), i % len(NC), NC[i % len(NC)]
                dve.wait_ge(S["agg0_hi"], i + 1)
                V.tensor_tensor(aT[:, 1, c, n0:n0 + w], tmp32[:, k, 0:w], aT[:, 0, c, n0:n0 + w],
                                ALU.subtract).then_inc(S["agg0_lo"], 1)

            for i in range(L0):
                c, (n0, w) = i // len(NC), NC[i % len(NC)]
                if i == SLOTS:
                    dve.wait_ge(S["invcol_ps"], 1)
                    V.tensor_copy(inv_col[:, 0:NT - 1], ps_a[1][:, IC:IC + NT - 1])
                    link(V.tensor_copy(inv_col[0:TAIL, NT - 1:NT], ps_a[1][0:TAIL, IC + NT - 1:IC + NT]))
                dve.wait_ge(S["ring_full"], i + 1)
                if i >= 3:
                    dve.wait_ge(S["agg0_lo"], i - 2)
                V.tensor_tensor(tmp32[:, i % 3, 0:w], ring[i % SLOTS][:, 0:w], inv_bc[:, n0:n0 + w], ALU.mult
                                ).then_inc(S["agg0_scaled"], 1)
                if i >= 1:
                    agg0_low(i - 1)
                if i == 3:
                    dve.wait_ge(S["Whi_ready"], 1)
                    w_low(0).then_inc(S["Wlo_ready"], 1)
                if i == 5:
                    gates_before_exp()
                if i == 7:
                    gates_after_exp()
                if i == 9:
                    w_max(1, 3, 2)
                    scales1(link)
                    V.memset(done_mark[:, 14:15], 0.0).then_inc(S["scale_ready"], 1)
            agg0_low(L0 - 1)

            base = chain[0]
            PER = 1 + 1 + 6 + 3

            def expert(e, last):
                cnt = [0]

                def step(ins):
                    cnt[0] += 1
                    ins.then_inc(S["dve"], 1)
                    dve.wait_ge(S["dve"], e * PER + base + cnt[0])

                V.tensor_copy(gate_now[:], gate[:, bass.ds(e, 1), :].rearrange("p o t -> p (o t)"))
                V.tensor_copy(sc[:, 6:7], sc[:, 7:8])
                V.tensor_scalar(sc[:, 10:11], sc[:, 1:2], 1.0 / HSCALE, None, ALU.mult)
                V.tensor_tensor(sc[:, 5:6], sc[:, 4:5], sc[:, 8:9], ALU.mult)
                step(V.tensor_scalar(bs[:], b0T[:, bass.ds(e * FC, FC)], sc[:, 7:8], None, ALU.mult))
                step(V.tensor_scalar(inv_s[:], inv_col[:], sc[:, 5:6], 1.0 / YSCALE, ALU.mult, ALU.mult))

                def l0_low(i):
                    c, k, (n0, w) = i // len(NC), i % len(NC), NC[i % len(NC)]
                    dve.wait_ge(S["l0_out"], e * L0 + i + 1)
                    V.tensor_tensor(h1T[:, 1, c, n0:n0 + w], tmp32[:, k, 0:w], h1T[:, 0, c, n0:n0 + w],
                                    ALU.subtract).then_inc(S["l0_lo"], 1)

                for i in range(L0):
                    c, k, w = i // len(NC), i % len(NC), NC[i % len(NC)][1]
                    dve.wait_ge(S["ring_full"], L0 + e * RING + i + 1)
                    dve.wait_ge(r_in[k], 16 * (e * FC + c + 1))
                    if i >= 3:
                        dve.wait_ge(S["l0_lo"], e * L0 + i - 2)
                    V.scalar_tensor_tensor(out=tmp32[:, k, 0:w], in0=ring[i % SLOTS][:, 0:w], scalar=sc[:, 10:11],
                                           in1=zt[:, k, 0:w], op0=ALU.mult, op1=ALU.add).then_inc(S["l0_sum"], 1)
                    if i >= 1:
                        l0_low(i - 1)
                    if i == 2:
                        dve.wait_ge(S["Whi_ready"], e * 2 + 2)
                        w_low(1)
                    if i == 5:
                        w_low(2).then_inc(S["Wlo_ready"], 1)
                l0_low(L0 - 1)
                for t in range(NT):
                    i, r = L0 + t, ROWS[t]
                    dve.wait_ge(S["y_hi"], e * NT + t + 1)
                    V.scalar_tensor_tensor(out=y[0:r, 1, t, :], in0=ring[i % SLOTS][0:r, :], scalar=YSCALE,
                                           in1=y[0:r, 0, t, :], op0=ALU.mult, op1=ALU.subtract
                                           ).then_inc(S["y_lo"], 1)
                dve.wait_ge(S["b1_in"], 16 * e + 16)

                def add_tile(t):
                    r = ROWS[t]
                    dve.wait_ge(S["relu_ready"], e * NT + t + 1)
                    V.tensor_tensor(acc[0:r, t, :], acc[0:r, t, :], zt[0:r, t % 3, :], ALU.add
                                    ).then_inc(S["tile_done"], 1)

                for t in range(NT):
                    r = ROWS[t]
                    dve.wait_ge(S["z_full"], e * NT + t + 1)
                    dve.wait_ge(S["tile_done"], CREDIT + e * NT + max(t - 2, 0))
                    V.scalar_tensor_tensor(out=zt[0:r, t % 3, :], in0=ps_z[t % 2][0:r, :],
                                           scalar=sc[0:r, 5:6], in1=bias1[0:r, :], op0=ALU.mult, op1=ALU.add
                                           ).then_inc(S["z_read"], 1)
                    dve.wait_ge(S["z_read"], CREDIT + e * NT + t + 1)
                    dve.wait_ge(S["a_full"], e * NT + t + 1)
                    V.scalar_tensor_tensor(out=zt[0:r, t % 3, :], in0=ps_a[t % 2][0:r, :],
                                           scalar=inv_s[0:r, t:t + 1], in1=zt[0:r, t % 3, :],
                                           op0=ALU.mult, op1=ALU.add).then_inc(S["t_ready"], 1)
                    if t >= 1:
                        add_tile(t - 1)
                    if t == 0 and not last:
                        w_max(e * 2 + 2, e * 3 + 4, 1)
                        scales0(e + 1, step)
                        V.memset(done_mark[:, 0:1], 0.0).then_inc(S["scale_ready"], 1)
                    if t == 2 and not last:
                        dve.wait_ge(S["Whi_ready"], e * 2 + 3)
                        w_low(0).then_inc(S["Wlo_ready"], 1)
                    if t == 6 and not last:
                        w_max(e * 2 + 3, e * 3 + 6, 2)
                        scales1(step)
                        V.memset(done_mark[:, 1:2], 0.0).then_inc(S["scale_ready"], 1)
                add_tile(NT - 1)
                assert last or cnt[0] == PER

            with dve.Fori(0, E - 1) as e:
                expert(e, False)
            expert(E - 1, True)

        @block.tensor
        def _(pe):
            T = nc.tensor
            pe.wait_ge(S["ident_ready"], 2)
            pe.wait_ge(S["edges_split"], 1)
            pe.wait_ge(S["edges_cast"], 3)
            for k, v in enumerate((dst_f, shi_f, slo_f)):
                for c in range(CH):
                    T.transpose(ring[k][0:EP, c * G:(c + 1) * G], v[:, c * EP:(c + 1) * EP], ident[0:G, 0:G])
            T.transpose(ring[3][0:EP, 0:G], mm_bc[:, 0, :], ident[0:G, 0:G])
            T.transpose(ring[3][0:EP, G:2 * G], mm_bc[:, 1, :], ident[0:G, 0:G]).then_inc(S["edges_T"], 1)

            pe.wait_ge(S["consts_in"], 16 * (2 + E))
            T.transpose(ps_a[1][:, 0:E * FC], b_rows[:], ident[0:E * FC, 0:E * FC]).then_inc(S["b0_ps"], 1)

            pe.wait_ge(S["flag_ready"], 1)
            need_slow = pe.value_load(flag_i[:], min_val=0, max_val=1)

            def gates(k, chunks=range(FC)):
                n0, w = NC[k]
                for c in chunks:
                    mm = T.matmul(ring[k][0:E, 0:w], gW[:, c, :], hT32[:, c, n0:n0 + w],
                                  start=(c == 0), stop=(c == FC - 1))
                if c == FC - 1:
                    mm.then_inc(S["gates_ps"], 1)

            for t in range(NT):
                r = ROWS[t]
                pe.wait_ge(S["xn_ready"], t + 1)
                if t >= 2:
                    pe.wait_ge(S["hThi_ready"], t - 1)
                for c in range(FC):
                    mm = T.transpose(ps_z[t % 2][:, c * P:c * P + r], zt[0:r, t % 3, c * P:(c + 1) * P],
                                     ident[0:r, 0:r])
                mm.then_inc(S["hT_ps"], 1)
                if t >= FIRST_FULL and t - FIRST_FULL < FC:
                    pe.wait_ge(S["hT32_ready"], FIRST_FULL)
                    gates(0, [t - FIRST_FULL])
            pe.wait_ge(S["hT32_ready"], (NC[1][0] + NC[1][1] + P - 1) // P)
            gates(1)


            def count(u, start, stop):
                for c in range(CH):
                    mm = T.matmul(ring[u][:, 0:AW], hotB[:, u, c, :], hotA[:, u, c, :],
                                  start=(start and c == 0), stop=(stop and c == CH - 1))
                return mm

            PAIRS = ((0, 0), (0, 1), (1, 0))

            def r_product(b, s, k):
                n0, w = NC[k]
                pe.wait_ge(S["hTlo_ready"], FIRST_FULL if k == 0 else NT - 2 + k)
                if k == 0:
                    pe.wait_ge(S["wb_lo"], b + 1)
                pe.wait_ge(S["r_evac"], b * len(NC) + k + 1)
                n = 0
                for f in range(FC):
                    for a, h in PAIRS:
                        mm = T.matmul(ps_r[k][:, 0:w], Wb16[:, s, a, f, :], hT[:, h, f, n0:n0 + w],
                                      start=(n == 0), stop=(n == 3 * FC - 1))
                        n += 1
                mm.then_inc(S["r_full"], 1)

            def pe_block(b, s, counts):
                for u in range(SLOTS):
                    if u < len(NC):
                        r_product(b, s, u)
                    if counts:
                        if u < len(NC) - 1:
                            pe.wait_ge(S["gT_ready"], u + 1)
                        pe.wait_ge(S["hot_ready"], b * SLOTS + u + 1)
                        pe.wait_ge(S["hotB_ready"], b * SLOTS + u + 1)
                        pe.wait_ge(S["added"], b * SLOTS + u + 1)
                        count(u, True, True).then_inc(S["counted"], 1)

            def pe_blocks(counts):
                with pe.Fori(0, NB // 2) as i:
                    pe_block(i * 2, 0, counts)
                    pe_block(i * 2 + 1, 1, counts)

            with pe.If(need_slow == 0):
                pe_blocks(True)
                pe.wait_ge(S["added"], SLOTS + G - 1)
            with pe.Else():
                pe.wait_ge(S["gT_ready"], 1)
                with pe.Fori(0, NWIN) as w:
                    pe.wait_ge(S["slow_read"], CREDIT + w)
                    pe.wait_ge(S["slow_hot"], w * G + 1)
                    count(0, True, False).then_inc(S["slow_counted"], 1)
                    with pe.Fori(1, G - 1) as g:
                        pe.wait_ge(S["slow_hot"], w * G + g + 1)
                        count(0, False, False).then_inc(S["slow_counted"], 1)
                    pe.wait_ge(S["slow_hot"], (w + 1) * G)
                    count(0, False, True).then_inc(S["slow_counted"], 1)
                pe_blocks(False)

            pe.wait_ge(S["hT32_ready"], NT)
            gates(len(NC) - 1)

            pe.wait_ge(S["C_ready"], 1)
            pe.wait_ge(S["ones_ready"], 1)
            pe.wait_ge(S["r_evac"], len(NC) * (NB + 1))
            for k, (n0, w) in enumerate(NC):
                T.matmul(ps_r[k][:, 0:w], ones16[:], C3[:, 0, n0:n0 + w], start=True, stop=False)
                with pe.If(need_slow != 0):
                    for t in range(NT):
                        T.matmul(ps_r[k][:, 0:w], ones16[0:ROWS[t], :], R3[0:ROWS[t], t, n0:n0 + w],
                                 start=False, stop=False)
                for t in range(1, NT):
                    mm = T.matmul(ps_r[k][:, 0:w], ones16[0:ROWS[t], :], C3[0:ROWS[t], t, n0:n0 + w],
                                  start=False, stop=(t == NT - 1))
                mm.then_inc(S["deg_ps"], 1)

            pe.wait_ge(S["gT_ready"], len(NC))
            pe.wait_ge(S["bmax_ready"], 1)
            for t in range(NT):
                mm = T.transpose(ps_a[1][0:ROWS[t], LG + t * E:LG + (t + 1) * E], gT[:, t * P:t * P + ROWS[t]],
                                 ident[0:E, 0:E])
            mm.then_inc(S["logits_ps"], 1)

            def inverse_columns():
                pe.wait_ge(S["inv_ready"], len(NC))
                for t in range(NT):
                    mm = T.matmul(ps_a[1][0:ROWS[t], IC + t:IC + t + 1], inv_bc[0:1, t * P:t * P + ROWS[t]],
                                  ident[0:1, 0:1], start=True, stop=True)
                mm.then_inc(S["invcol_ps"], 1)

            pe.wait_ge(S["h16lo_ready"], NT)
            for i in range(L0):
                c, (n0, w) = i // len(NC), NC[i % len(NC)]
                if i == SLOTS:
                    inverse_columns()
                if i >= SLOTS:
                    pe.wait_ge(S["agg0_scaled"], i - SLOTS + 1)

                def part(k, t, M3, start, stop):
                    r = ROWS[t]
                    return T.matmul(ring[i % SLOTS][:, 0:w], y[0:r, k, t, c * P:(c + 1) * P],
                                    M3[0:r, t, n0:n0 + w], start=start, stop=stop)

                part(0, 0, C3, True, False)
                with pe.If(need_slow != 0):
                    for t in range(NT):
                        part(0, t, R3, False, False)
                        part(1, t, R3, False, False)
                part(1, 0, C3, False, False)
                for t in range(1, NT):
                    part(0, t, C3, False, False)
                    mm = part(1, t, C3, False, t == NT - 1)
                mm.then_inc(S["ring_full"], 1)

            def expert(e, last):
                pe.wait_ge(S["Wlo_ready"], e * 2 + 1)
                pe.wait_ge(S["y_lo"], CREDIT + e * NT)
                for i in range(L0):
                    c, (n0, w) = i // len(NC), NC[i % len(NC)]
                    if i < len(NC):
                        pe.wait_ge(S["agg0_lo"], L0 - len(NC) + i + 1)
                    if i >= SLOTS:
                        pe.wait_ge(S["l0_sum"], e * L0 + i - SLOTS + 1)
                    n = 0
                    for k in range(FC):
                        for a, b in PAIRS:
                            mm = T.matmul(ring[i % SLOTS][:, 0:w], W16a[:, a, k, c * P:(c + 1) * P],
                                          aT[:, b, k, n0:n0 + w], start=(n == 0), stop=(n == 3 * FC - 1))
                            n += 1
                    mm.then_inc(S["ring_full"], 1)
                pe.wait_ge(S["Wlo_ready"], e * 2 + 2)
                for t in range(NT):
                    i, r = L0 + t, ROWS[t]
                    ready = L0 - sum(n0 >= t * P + r for n0, _ in NC)
                    pe.wait_ge(S["l0_lo"], e * L0 + ready)
                    if t < SLOTS:
                        pe.wait_ge(S["l0_sum"], e * L0 + i - SLOTS + 1)
                    else:
                        pe.wait_ge(S["y_lo"], CREDIT + e * NT + t - SLOTS + 1)
                    n = 0
                    for k in range(FC):
                        for a, b in PAIRS:
                            mm = T.matmul(ring[i % SLOTS][0:r, :], h1T[:, b, k, t * P:t * P + r],
                                          W16b[:, a, 0, k, :], start=(n == 0), stop=(n == 3 * FC - 1))
                            n += 1
                    mm.then_inc(S["ring_full"], 1)
                for t in range(NT):
                    r = ROWS[t]
                    if t < 2:
                        pe.wait_ge(S["t_ready"], CREDIT + e * NT)
                    else:
                        pe.wait_ge(S["z_read"], CREDIT + e * NT + t - 1)
                    n = 0
                    for k in range(FC):
                        for a, b in PAIRS:
                            mm = T.matmul(ps_z[t % 2][0:r, :], h1T[:, b, k, t * P:t * P + r],
                                          W16b[:, a, 1, k, :], start=(n == 0), stop=(n == 3 * FC - 1))
                            n += 1
                    mm.then_inc(S["z_full"], 1)
                    if t == 0:
                        pe.wait_ge(S["y_lo"], CREDIT + (e + 1) * NT)
                    if t >= 2:
                        pe.wait_ge(S["t_ready"], CREDIT + e * NT + t - 1)

                    def part(k, s, M3, start, stop):
                        q = ROWS[s]
                        return T.matmul(ps_a[t % 2][0:r, :], M3[0:q, s, t * P:t * P + r], y[0:q, k, s, :],
                                        start=start, stop=stop)

                    part(0, 0, C3, True, False)
                    with pe.If(need_slow != 0):
                        for s in range(NT):
                            part(0, s, R3, False, False)
                            part(1, s, R3, False, False)
                    part(1, 0, C3, False, False)
                    for s in range(1, NT):
                        part(0, s, C3, False, False)
                        mm = part(1, s, C3, False, s == NT - 1)
                    mm.then_inc(S["a_full"], 1)

            with pe.Fori(0, E - 1) as e:
                expert(e, False)
            expert(E - 1, True)


_INS = ["x", "src", "dst", "L0_gnn_gate_W", "L0_gnn_gate_b", "L0_gnn_Wl", "L0_gnn_bl", "L0_gnn_Wr"]
_OUTS = [((1250, 512), "float32")]


def kernel(**inputs):
    import numpy as _np
    import concourse.bacc as _bacc
    from concourse import mybir as _mybir
    from concourse.bass_utils import run_bass_kernel_spmd as _run

    nc = _bacc.Bacc("TRN2", target_bir_lowering=False, num_devices=1)
    arrays, args = {}, []
    for name in _INS:
        a = _np.ascontiguousarray(inputs[name])
        arrays[f"in_{name}_dram"] = a
        args.append(nc.dram_tensor(f"in_{name}_dram", a.shape, _mybir.dt.from_np(a.dtype), kind="ExternalInput").ap())
    for i, (shape, dtype) in enumerate(_OUTS):
        dt = _mybir.dt.from_np(_np.dtype(dtype))
        args.append(nc.dram_tensor(f"out_{i}_dram", shape, dt, kind="ExternalOutput").ap())
    sage_moe_kernel(nc, *args)
    r = _run(nc, [arrays], core_ids=[0])
    return r.results[0]["out_0_dram"]
```
